# Optimizing a Trainium2 kernel written in Bass

```python
import numpy as np
import jax
import jax.numpy as jnp

def _softmax(x, axis=-1):
    return jax.nn.softmax(x, axis=axis)

def _gelu(x):
    return jax.nn.gelu(x, approximate=True)

def _silu(x):
    return jax.nn.silu(x)

def _sigmoid(x):
    return jax.nn.sigmoid(x)

def _layernorm(x, axis=-1, eps=1e-05):
    m = jnp.mean(x, axis=axis, keepdims=True)
    v = jnp.var(x, axis=axis, keepdims=True)
    return (x - m) / jnp.sqrt(v + eps)

def _scatter_add(tgt, idx, src, axis=0):
    return tgt.at[idx].add(src)

def _segment_sum(src, seg, n):
    return jax.ops.segment_sum(src, seg, n)
kernel_name = 'mk_conv_preact_d2_conv_nhwc256_r4_a4f553'

def setup_inputs(seed: int=0):
    np.random.seed(seed)
    _w = jnp.asarray

    def _rec_inputs():
        import jax
        import jax.numpy as jnp
        _gk = jax.random.key(seed)
        x = -0.000125 + 0.9999 * jax.random.normal(jax.random.fold_in(_gk, 1), (8, 32, 32, 64), jnp.float32)
        return x
    x = _rec_inputs()

    def _L0_conv_setup():
        import jax, jax.numpy as jnp
        import numpy as np
        B, H, W, C = (8, 32, 32, 64)
        K, DT, EPS = (5, 0.2, 0.001)
        LAM2 = 4.0

        def _dwconv(x, w):
            k = w.reshape(3, 3, 1, C)
            return jax.lax.conv_general_dilated(x, k, (1, 1), 'SAME', dimension_numbers=('NHWC', 'HWIO', 'NHWC'), feature_group_count=C)

        def _bn(x, gamma, beta, mean, var):
            return (x - mean) * jax.lax.rsqrt(var + EPS) * gamma + beta

        def _sobel(x):
            xp = jnp.pad(x, ((0, 0), (1, 1), (1, 1), (0, 0)), mode='reflect')
            top, mid, bot = (xp[:, :-2], xp[:, 1:-1], xp[:, 2:])
            gy = bot[:, :, :-2] + 2 * bot[:, :, 1:-1] + bot[:, :, 2:] - (top[:, :, :-2] + 2 * top[:, :, 1:-1] + top[:, :, 2:])
            gx = top[:, :, 2:] + 2 * mid[:, :, 2:] + bot[:, :, 2:] - (top[:, :, :-2] + 2 * mid[:, :, :-2] + bot[:, :, :-2])
            return (gy, gx)
        key = jax.random.key(seed)
        ks = jax.random.split(key, 6)
        f = jnp.float32
        d = {}
        d['s0'] = jax.random.normal(ks[0], (B, H, W, C), f)
        d['wg'] = jax.random.normal(ks[1], (3, 3, C), f) * 0.1
        d['wg1'] = jax.random.normal(ks[2], (3, 3, C), f) * 0.1
        for i, p in enumerate(['g', 'g1', 'out']):
            k4 = jax.random.split(ks[3 + i], 4)
            d[p + '_gamma'] = 1.0 + 0.1 * jax.random.normal(k4[0], (C,), f)
            d[p + '_beta'] = 0.1 * jax.random.normal(k4[1], (C,), f)
            d[p + '_mean'] = 0.1 * jax.random.normal(k4[2], (C,), f)
            d[p + '_var'] = 0.5 + jax.random.uniform(k4[3], (C,), f)
        return d
    _L0_conv_all = _L0_conv_setup()
    _L0_conv_in = {k: v for k, v in _L0_conv_all.items() if k in ('wg', 'wg1', 'g_gamma', 'g_beta', 'g_mean', 'g_var', 'g1_gamma', 'g1_beta', 'g1_mean', 'g1_var', 'out_gamma', 'out_beta', 'out_mean', 'out_var')}
    del _L0_conv_all

    def _L1_conv_setup():
        import jax, jax.numpy as jnp
        import numpy as np

        def _threshold(w):
            return 0.7 * jnp.mean(jnp.abs(w))

        def _compute_alpha(w):
            t = _threshold(w)
            kept = jnp.where(w > t, w, 0.0) + jnp.where(w < -t, w, 0.0)
            kept_abs = jnp.abs(kept)
            n = jnp.sum((kept_abs > 0).astype(w.dtype))
            return jnp.sum(kept_abs) / n

        def _ternary(w):
            t = _threshold(w)
            return jnp.sign(jnp.sign(w + t) + jnp.sign(w - t))
        key = jax.random.key(seed)
        k1, k2 = jax.random.split(key)
        x = jax.random.normal(k1, (16, 56, 56, 64), dtype=jnp.float32)
        W = jax.random.normal(k2, (3, 3, 64, 64), dtype=jnp.float32) * 0.02
        b = jnp.zeros((64,), dtype=jnp.float32)
        return {'x': x, 'W': W, 'b': b}
    _L1_conv_all = _L1_conv_setup()
    _L1_conv_in = {k: v for k, v in _L1_conv_all.items() if k in ('W', 'b')}
    del _L1_conv_all
    return {'x': x, 'L0_conv_wg': _L0_conv_in['wg'], 'L0_conv_wg1': _L0_conv_in['wg1'], 'L0_conv_g_gamma': _L0_conv_in['g_gamma'], 'L0_conv_g_beta': _L0_conv_in['g_beta'], 'L0_conv_g_mean': _L0_conv_in['g_mean'], 'L0_conv_g_var': _L0_conv_in['g_var'], 'L0_conv_g1_gamma': _L0_conv_in['g1_gamma'], 'L0_conv_g1_beta': _L0_conv_in['g1_beta'], 'L0_conv_g1_mean': _L0_conv_in['g1_mean'], 'L0_conv_g1_var': _L0_conv_in['g1_var'], 'L0_conv_out_gamma': _L0_conv_in['out_gamma'], 'L0_conv_out_beta': _L0_conv_in['out_beta'], 'L0_conv_out_mean': _L0_conv_in['out_mean'], 'L0_conv_out_var': _L0_conv_in['out_var'], 'L1_conv_W': _L1_conv_in['W'], 'L1_conv_b': _L1_conv_in['b']}

def reference(x, L0_conv_wg, L0_conv_wg1, L0_conv_g_gamma, L0_conv_g_beta, L0_conv_g_mean, L0_conv_g_var, L0_conv_g1_gamma, L0_conv_g1_beta, L0_conv_g1_mean, L0_conv_g1_var, L0_conv_out_gamma, L0_conv_out_beta, L0_conv_out_mean, L0_conv_out_var, L1_conv_W, L1_conv_b):
    import jax
    import jax.numpy as jnp

    def _L0_conv_ref(s0, wg, wg1, g_gamma, g_beta, g_mean, g_var, g1_gamma, g1_beta, g1_mean, g1_var, out_gamma, out_beta, out_mean, out_var):
        import jax, jax.numpy as jnp
        import numpy as np
        B, H, W, C = (8, 32, 32, 64)
        K, DT, EPS = (5, 0.2, 0.001)
        LAM2 = 4.0

        def _dwconv(x, w):
            k = w.reshape(3, 3, 1, C)
            return jax.lax.conv_general_dilated(x, k, (1, 1), 'SAME', dimension_numbers=('NHWC', 'HWIO', 'NHWC'), feature_group_count=C)

        def _bn(x, gamma, beta, mean, var):
            return (x - mean) * jax.lax.rsqrt(var + EPS) * gamma + beta

        def _sobel(x):
            xp = jnp.pad(x, ((0, 0), (1, 1), (1, 1), (0, 0)), mode='reflect')
            top, mid, bot = (xp[:, :-2], xp[:, 1:-1], xp[:, 2:])
            gy = bot[:, :, :-2] + 2 * bot[:, :, 1:-1] + bot[:, :, 2:] - (top[:, :, :-2] + 2 * top[:, :, 1:-1] + top[:, :, 2:])
            gx = top[:, :, 2:] + 2 * mid[:, :, 2:] + bot[:, :, 2:] - (top[:, :, :-2] + 2 * mid[:, :, :-2] + bot[:, :, :-2])
            return (gy, gx)
        fsrc = s0
        h = s0
        h0 = fsrc
        g = jax.nn.relu(_bn(_dwconv(h, wg), g_gamma, g_beta, g_mean, g_var))
        g1 = jax.nn.relu(_bn(_dwconv(h, wg1), g1_gamma, g1_beta, g1_mean, g1_var))
        gy, gx = _sobel(h)
        Dx = 1.0 / (gy * gy / LAM2 + 1.0)
        Dy = 1.0 / (gx * gx / LAM2 + 1.0)
        ux = 0.5 * (jnp.roll(g, 1, axis=2) - jnp.roll(g, -1, axis=2))
        vy = 0.5 * (jnp.roll(g1, 1, axis=3) - jnp.roll(g1, -1, axis=3))
        Ax, Ay = (g * DT, g1 * DT)
        Bx, By = (Dx * DT, Dy * DT)
        E = (ux + vy) * DT
        D = 1.0 / (1.0 + 2.0 * Bx + 2.0 * By)
        cm_x, cp_x = (-Ax + 2.0 * Bx, Ax + 2.0 * Bx)
        cm_y, cp_y = (-Ay + 2.0 * By, Ay + 2.0 * By)
        c0 = 1.0 - 2.0 * Bx - 2.0 * By
        for _ in range(K):
            prev = h
            h = D * (c0 * h0 - 2.0 * E * h + cm_x * jnp.roll(h, 1, axis=2) + cp_x * jnp.roll(h, -1, axis=2) + cm_y * jnp.roll(h, 1, axis=3) + cp_y * jnp.roll(h, -1, axis=3))
            h = h + D * (2.0 * DT) * fsrc
            h0 = prev
        return jax.nn.relu(_bn(h, out_gamma, out_beta, out_mean, out_var))

    def _L1_conv_ref(x, W, b):
        import jax, jax.numpy as jnp
        import numpy as np

        def _threshold(w):
            return 0.7 * jnp.mean(jnp.abs(w))

        def _compute_alpha(w):
            t = _threshold(w)
            kept = jnp.where(w > t, w, 0.0) + jnp.where(w < -t, w, 0.0)
            kept_abs = jnp.abs(kept)
            n = jnp.sum((kept_abs > 0).astype(w.dtype))
            return jnp.sum(kept_abs) / n

        def _ternary(w):
            t = _threshold(w)
            return jnp.sign(jnp.sign(w + t) + jnp.sign(w - t))
        alpha = _compute_alpha(W)
        w_q = alpha * _ternary(W)
        y = jax.lax.conv_general_dilated(x, w_q, window_strides=(1, 1), padding='SAME', dimension_numbers=('NHWC', 'HWIO', 'NHWC'))
        return jax.nn.relu(y + b)

    def _gn(v, G=32, eps=1e-05):
        B_, H_, W_, C_ = v.shape
        g = v.reshape(B_, H_, W_, G, C_ // G)
        m = jnp.mean(g, axis=(1, 2, 4), keepdims=True)
        s = jnp.var(g, axis=(1, 2, 4), keepdims=True)
        return ((g - m) / jnp.sqrt(s + eps)).reshape(v.shape)

    def _ln_c(v, eps=1e-06):
        m = jnp.mean(v, axis=-1, keepdims=True)
        s = jnp.var(v, axis=-1, keepdims=True)
        return (v - m) / jnp.sqrt(s + eps)

    def _ln_t(v, eps=1e-05):
        m = jnp.mean(v, axis=-1, keepdims=True)
        s = jnp.var(v, axis=-1, keepdims=True)
        return (v - m) / jnp.sqrt(s + eps)

    def _to_tokens(v):
        B_, H_, W_, C_ = v.shape
        return v.reshape(B_, H_ * W_, C_)

    def _from_tokens(t, like):
        return t.reshape(like.shape)
    x = x + _L0_conv_ref(_gn(x), L0_conv_wg, L0_conv_wg1, L0_conv_g_gamma, L0_conv_g_beta, L0_conv_g_mean, L0_conv_g_var, L0_conv_g1_gamma, L0_conv_g1_beta, L0_conv_g1_mean, L0_conv_g1_var, L0_conv_out_gamma, L0_conv_out_beta, L0_conv_out_mean, L0_conv_out_var)
    x = x + _L1_conv_ref(_gn(x), L1_conv_W, L1_conv_b)
    return x

_drawn_inputs = setup_inputs


def setup_inputs(seed=0):
    import zlib

    import numpy as np

    out = dict(_drawn_inputs(seed))
    spreads = {'L1_conv_b': (0.0, 0.1)}
    factors = {'L0_conv_g_gamma': 8.0,
     'L0_conv_g_beta': 3.87,
     'L0_conv_g_mean': 3.414,
     'L0_conv_g_var': 4.706,
     'L0_conv_g1_gamma': 8.0,
     'L0_conv_g1_beta': 3.509,
     'L0_conv_g1_mean': 3.016,
     'L0_conv_g1_var': 6.689}
    for name, (base, spread) in spreads.items():
        noise = np.random.default_rng([zlib.crc32(name.encode()), seed]).standard_normal(out[name].shape)
        drawn = base * np.exp(spread * noise) if base else spread * noise
        out[name] = jnp.asarray(drawn.astype(out[name].dtype))
    for name, factor in factors.items():
        out[name] = (out[name] * factor).astype(out[name].dtype)
    return out
```

```python
from contextlib import ExitStack

from concourse import mybir

B, H, W, C = 8, 32, 32, 64
TILES = 2
BT = B // TILES
N = W * C
HALF = N // 2
BANK = 512
CP = 4
CG = C // CP
PITCH = C + 2
ROWS = W + 2
STEPS = 5
DT = 0.2
BN_EPS, GN1_EPS, GN2_EPS = 1e-3, 1e-5, 1e-5
GROUPS = 32
PER_GROUP = H * W * (C // GROUPS)
PAIRS = W // 2
HP = H + 2
NCOEF = 7
A0, AE, FS, AXM, AXP, AYM, AYP = 1, 3, 0, 6, 4, 2, 5
RING = 3
SLOTS = 4
FAR = 200



def job_table():
    early = ["wtaps", "mean_0", "bnrow", "var_0", "mean_1", "t2_0_0", "t2_0_1",
             "gy_0_0", "gy_0_1", "gx_0_0", "gx_0_1", "wsum", "var_1",
             "cv_0_0_0", "cv_0_0_1", "cv_0_1_0", "bk_0_0_0", "cv_0_1_1", "bk_0_0_1", "t2_1_0", "t2_1_1",
             "bk_0_1_0", "bk_0_1_1", "alpha",
             "cv_1_0_0", "cv_1_0_1", "cv_1_1_0", "bk_1_0_0", "cv_1_1_1", "bk_1_0_1", "bk_1_1_0",
             "gy_1_0", "gy_1_1", "bk_1_1_1", "gx_1_0", "gx_1_1"]
    jobs = [(name, i % SLOTS) for i, name in enumerate(early)]

    def halves(name, t):
        return [(f"{name}_{t}_{h}", 2 * t + h) for h in range(2)]

    for k in range(STEPS):
        for t in range(TILES):
            if (k, t) == (STEPS - 1, 1):
                jobs += halves("th", 0) + halves("tx", 0)
            jobs += [(f"acc_{k}_{t}_{h}", 2 * t + h) for h in range(2)]
    jobs += [("mean2_0", 0)] + halves("th", 1) + halves("tx", 1) + [("var2_0", 1), ("mean2_1", 2)]
    jobs += halves("cf", 0) + [("var2_1", 3)] + halves("tb", 0) + halves("cf", 1) + halves("tb", 1)
    return jobs


def network(nc, x, wg, wg1, bn_rows, out_cols, conv_w, out):
    f32, f32r, i32 = mybir.dt.float32, mybir.dt.float32r, mybir.dt.int32
    ALU, ACT, AX = mybir.AluOpType, mybir.ActivationFunctionType, mybir.AxisListType

    jobs = job_table()
    job_no = {name: i for i, (name, _) in enumerate(jobs)}
    slot_of = dict(jobs)
    uses_before, seen = {}, [0] * SLOTS
    for name, slot in jobs:
        uses_before[name] = seen[slot]
        seen[slot] += 1

    with ExitStack() as ctx:
        def sb(name, shape, dt=f32):
            return ctx.enter_context(nc.sbuf_tensor(name, shape, dt))

        def sem(name):
            return ctx.enter_context(nc.semaphore(name))

        coef = sb("coef", [128, TILES, NCOEF, N])
        state = sb("state", [128, TILES, 2, ROWS, PITCH])
        ring = sb("ring", [128, RING, N])
        hi = sb("hi", [128, (PAIRS + 1) * BT * HP], f32r)
        lo = sb("lo", [128, (PAIRS + 1) * BT * HP], f32r)
        sobel_m = sb("sobel_m", [128, 4, 128], f32r)
        dense_m = sb("dense_m", [128, 2, 3, 128], f32r)
        ident = sb("ident", [128, 128])
        block = sb("block", [128, CP, 32])
        smooth = sb("smooth", [128, CP, 32])
        diff = sb("diff", [128, CP, 32])
        near = sb("near", [128, 3, CP, 32])
        tapmask = sb("tapmask", [128, 3, 32])
        spread4 = sb("spread4", [CP, CP, 32])
        pairavg = sb("pairavg", [128, 2, GROUPS, 2])
        ones = sb("ones", [128, 128])
        taps4 = sb("taps4", [CP, 2, 9, CG])
        taps = sb("taps", [128, 2 * 9 * CG])
        bn4 = sb("bn4", [CP, 4, 2 * CG])
        bn4w = sb("bn4w", [CP, 3, 2 * CG])
        bn4o = sb("bn4o", [CP, 2, 2 * CG])
        bnp = sb("bnp", [128, 2, 2, CG])
        outp = sb("outp", [128, 5])
        outw = sb("outw", [128, 4])
        gsum = sb("gsum", [128, TILES, 4, GROUPS])
        rs_in = sb("rs_in", [128, GROUPS])
        rs_ln = sb("rs_ln", [128, GROUPS])
        rs_y = sb("rs_y", [128, GROUPS])
        rs_t = sb("rs_t", [128, 3, GROUPS])
        wred = sb("wred", [128, 8])
        stats = sb("stats", [128, BT, 6])
        mv = sb("mv", [128, TILES, BT, 2])
        minus16 = sb("minus16", [128, 1])
        gn2 = sb("gn2", [128, TILES, 6, BT])
        psum = ctx.enter_context(nc.psum_tensor("psum", [128, SLOTS, HALF], f32))

        x_in = [ring[:, t, :] for t in range(TILES)]
        square = ring[:, 2, :]
        scratch = ring[:, 2, :]
        compact = coef[:, 0, 0:2, :].rearrange("p a n -> p (a n)")[:, 0:96 * 32].rearrange("p (m w) -> p m w", w=32)
        taps_m = coef[:, 1, 0:6, :].rearrange("p a n -> p (a n)").rearrange("p (m n) -> p m n", n=128)
        wl = coef[:, 1, 6, 0:9 * C]
        wabs = coef[:, 1, 6, 9 * C:18 * C]
        wtern = coef[:, 1, 6, 18 * C:27 * C]
        sT = [state[:, t, 1, :, :].rearrange("p r q -> p (r q)")[:, 0:N] for t in range(TILES)]
        gT = [ring[:, 0, :], ring[:, 1, :]]
        gN = [coef[:, t, 6, :] for t in range(TILES)]
        g1N = sT

        def h_at(t, k, dw=0, dc=0, w0=0, w1=W):
            return state[:, t, k % 2, 1 + dw + w0:1 + dw + w1, 1 + dc:1 + dc + C]

        def wc(ap):
            return ap.rearrange("p (w c) -> p w c", c=C)

        def half(ap, h):
            return ap[:, h * HALF:(h + 1) * HALF]

        def slot_ap(name):
            return psum[:, slot_of[name], :]

        taps_in, bn_in, outp_in, wl_in = sem("taps_in"), sem("bn_in"), sem("outp_in"), sem("wl_in")
        x_loaded = [sem("x_loaded0"), sem("x_loaded1")]
        x_again = [sem("x_again0"), sem("x_again1")]
        out_stored = sem("out_stored")
        pe_job = sem("pe_job")
        slot_free = [sem(f"slot_free{q}") for q in range(SLOTS)]
        pool_step, dve_step, act_step = sem("pool_step"), sem("dve_step"), sem("act_step")
        spread_ready, near_ready, ident_ready, sobel_src = (sem(n) for n in (
            "spread_ready", "near_ready", "ident_ready", "sobel_src"))
        ones_ready, pairavg_ready, zero_ready = sem("ones_ready"), sem("pairavg_ready"), sem("zero_ready")
        compact_ready, taps_m_ready = sem("compact_ready"), sem("taps_m_ready")
        xsum_ready, xm_ready, sq_ready, vsum_ready = (sem(n) for n in (
            "xsum_ready", "xm_ready", "sq_ready", "vsum_ready"))
        s_ready, s_hi, s_lo, s_halo = sem("s_ready"), sem("s_hi"), sem("s_lo"), sem("s_halo")
        s_reordered, den_const = sem("s_reordered"), sem("den_const")
        rs_asked, rs_given = sem("rs_asked"), sem("rs_given")
        bn4_ready, outw_ready = sem("bn4_ready"), sem("outw_ready")
        sobel_m_ready, dense_m_ready = sem("sobel_m_ready"), sem("dense_m_ready")
        c14_ready, u_ready, y_ready, sb_ready, d_ready, coef_ready = (sem(n) for n in (
            "c14_ready", "u_ready", "y_ready", "sb_ready", "d_ready", "coef_ready"))
        product, ring_free = sem("product"), sem("ring_free")
        halo_ready, s_scaled = sem("halo_ready"), sem("s_scaled")
        wabs_ready, kept_ready, alpha_ready, tern_ready = (sem(n) for n in (
            "wabs_ready", "kept_ready", "alpha_ready", "tern_ready"))
        mv_ready, q_ready, norm_ready, xn_ready, xh_ready, xl_ready = (sem(n) for n in (
            "mv_ready", "q_ready", "norm_ready", "xn_ready", "xh_ready", "xl_ready"))
        pads_ready, odd_ready, sum_ready = sem("pads_ready"), sem("odd_ready"), sem("sum_ready")

        def wait_job(eng, name):
            eng.wait_ge(pe_job, job_no[name] + 1)

        def wait_reader(eng, name):
            eng.wait_ge(slot_free[slot_of[name]], uses_before[name] + 1)

        def frees(ins, name):
            ins.then_inc(slot_free[slot_of[name]], 1)

        def products_of(k):
            return 4 if k == 0 else 5

        def products_through(k, t):
            return TILES * sum(products_of(kk) for kk in range(k)) + products_of(k) * (t + 1)

        x_nat = x.rearrange("(t b) h w c -> t (b h) (w c)", t=TILES)
        out_nat = out.rearrange("(t b) h w c -> t (b h) (w c)", t=TILES)

        blk = ctx.enter_context(nc.Block())

        @blk.sync
        def _(sp):
            for conv, src in enumerate((wg, wg1)):
                sp.dma_start(taps4[:, conv, :, :],
                             src.rearrange("y x (a g) -> a (y x) g", g=CG)).then_inc(taps_in, 16)
            for t in range(TILES):
                sp.dma_start(x_in[t], x_nat[t]).then_inc(x_loaded[t], 16)
            for k in range(2):
                sp.dma_start(wl[64 * k:64 * k + 64, :].rearrange("i (k o) -> i k o", o=C),
                             conv_w.rearrange("y x i o -> i (y x) o")).then_inc(wl_in, 16)
            for i, col in enumerate(out_cols):
                for k in range(2):
                    sp.dma_start(outp[64 * k:64 * k + 64, i:i + 1], col).then_inc(outp_in, 16)
            for t in range(TILES):
                sp.wait_ge(product, products_through(STEPS - 1, t) - products_of(STEPS - 1) + 1)
                sp.dma_start(coef[:, t, 1, :], x_nat[t]).then_inc(x_again[t], 16)
            for t in range(TILES):
                for h in range(2):
                    wait_reader(sp, f"tb_{t}_{h}")
                    sp.dma_start(half(out_nat[t], h), half(coef[:, t, 4, :], h)).then_inc(out_stored, 16)
            sp.wait_ge(out_stored, 16 * 2 * TILES)

        @blk.gpsimd
        def _(pool):
            steps = [0]

            def then(ins):
                steps[0] += 1
                ins.then_inc(pool_step, 1)
                pool.wait_ge(pool_step, steps[0])

            def select(ap, pattern, base, mult, fill, op=ALU.not_equal):
                return nc.gpsimd.affine_select(out=ap, in_=ap, pattern=pattern, compare_op=op, fill=fill, base=base,
                                               channel_multiplier=mult)

            def times_block(ap):
                return nc.gpsimd.tensor_tensor(ap, ap, block[:, :, :], ALU.mult)

            nc.gpsimd.memset(minus16[:, :], -(2 * DT) ** 2).then_inc(den_const, 1)
            then(nc.gpsimd.memset(spread4[:, :, :], 0.0))
            select(spread4[:, :, :], [[-1, CP], [0, 32]], 0, 1, 1.0).then_inc(spread_ready, 1)
            then(nc.gpsimd.memset(block[:, :, :], 1.0))
            then(select(block[:, :, :], [[-32, CP], [0, 32]], 0, 1, 0.0, ALU.is_ge))
            then(select(block[:, :, :], [[32, CP], [0, 32]], 31, -1, 0.0, ALU.is_ge))
            then(nc.gpsimd.memset(near[:, :, :, :], 0.0))
            for d in range(3):
                then(select(near[:, d, :, :], [[-32, CP], [-1, 32]], 1 - d, 1, 1.0))
                times_block(near[:, d, :, :]).then_inc(near_ready, 1)
            nc.gpsimd.memset(coef[:, 1, 0:6, :].rearrange("p a n -> p (a n)"), 0.0).then_inc(zero_ready, 1)
            then(nc.gpsimd.memset(ident[:, :], 0.0))
            select(ident[:, :], [[-1, 128]], 0, 1, 1.0).then_inc(ident_ready, 1)
            then(nc.gpsimd.memset(smooth[:, :, :], 0.0))
            then(select(smooth[:, :, :], [[-32, CP], [-1, 32]], 0, 1, 2.0))
            then(select(smooth[:, :, :], [[-32, CP], [-1, 32]], -1, 1, 1.0))
            then(select(smooth[:, :, :], [[-32, CP], [-1, 32]], 1, 1, 1.0))
            then(times_block(smooth[:, :, :]))
            then(select(smooth[:, :, :], [[-32, CP], [FAR, 32]], -1, 1, 2.0))
            select(smooth[:, :, :], [[-32, CP], [FAR, 32]], -30 - 31 * FAR, 1, 2.0).then_inc(sobel_src, 1)
            then(nc.gpsimd.memset(diff[:, :, :], 0.0))
            then(select(diff[:, :, :], [[-32, CP], [-1, 32]], -1, 1, 1.0))
            then(select(diff[:, :, :], [[-32, CP], [-1, 32]], 1, 1, -1.0))
            then(times_block(diff[:, :, :]))
            then(select(diff[:, :, :], [[0, CP], [1, 32]], 0, 0, 0.0, ALU.is_gt))
            select(diff[:, :, :], [[0, CP], [-1, 32]], 31, 0, 0.0, ALU.is_gt).then_inc(sobel_src, 1)
            nc.gpsimd.memset(ones[:, :], 1.0).then_inc(ones_ready, 1)
            nc.gpsimd.memset(dense_m[:, :, :, :].bitcast(f32), 0.0).then_inc(zero_ready, 1)
            then(nc.gpsimd.memset(pairavg[:, :, :, :], 0.25))
            for k in range(2):
                part = pairavg[64 * k:64 * k + 64, :, :, :]
                then(select(part, [[0, 2], [-2, GROUPS], [0, 2]], 0, 1, 0.0, ALU.is_ge))
                select(part, [[0, 2], [2, GROUPS], [0, 2]], 1, -1, 0.0, ALU.is_ge).then_inc(pairavg_ready, 1)
                pool.wait_ge(pairavg_ready, k + 1)
            wait_job(pool, "gx_1_1")
            nc.gpsimd.memset(hi[:, :].bitcast(f32), 0.0).then_inc(pads_ready, 1)
            nc.gpsimd.memset(lo[:, :].bitcast(f32), 0.0).then_inc(pads_ready, 1)

        @blk.scalar
        def _(act):
            steps, asked = [0], [0]

            def then(ins):
                steps[0] += 1
                ins.then_inc(act_step, 1)
                act.wait_ge(act_step, steps[0])

            def copy(dst, src, func=ACT.Copy, **kw):
                return nc.scalar.activation(dst, src, func, **kw)

            def rsqrt_first(p, n):
                asked[0] += 1
                act.wait_ge(rs_asked, asked[0])
                then(copy(rs_ln[0:p, 0:n], rs_in[0:p, 0:n], ACT.Ln))
                copy(rs_y[0:p, 0:n], rs_ln[0:p, 0:n], ACT.Exp, scale=-0.5).then_inc(rs_given, 1)

            def square_of(t):
                act.wait_ge(xm_ready, t + 1)
                copy(wc(square), h_at(t, 0), ACT.Square).then_inc(sq_ready, 1)

            def wrap(t, k, done):
                s = state[:, t, k % 2, :, :]
                copy(s[:, 0, 1:1 + C], s[:, W, 1:1 + C]).then_inc(done, 1)
                copy(s[:, W + 1, 1:1 + C], s[:, 1, 1:1 + C]).then_inc(done, 1)
                copy(s[:, 1:1 + W, 0:1], s[:, 1:1 + W, C:C + 1]).then_inc(done, 1)
                copy(s[:, 1:1 + W, C + 1:C + 2], s[:, 1:1 + W, 1:2]).then_inc(done, 1)

            def split_hi(t):
                act.wait_ge(s_ready, t + 1)
                if t:
                    wait_job(act, "gx_0_1")
                copy(wc(hi[:, 0:N]), h_at(t, 0)).then_inc(s_hi, 1)

            def reorder(t):
                act.wait_ge(s_ready, t + 1)
                copy(sT[t].rearrange("p (g a w) -> p g a w", a=CP, w=W),
                     h_at(t, 0).rearrange("p w (a g) -> p g a w", g=CG)).then_inc(s_reordered, 1)

            def to_depthwise(t, h):
                wait_job(act, f"t2_{t}_1")
                frees(copy(half(sT[t], h), slot_ap(f"t2_{t}_{h}")), f"t2_{t}_{h}")

            def sobel_square(t, g, h):
                name = f"{('gy', 'gx')[g]}_{t}_{h}"
                wait_job(act, name)
                frees(copy(half(coef[:, t, g, :], h), slot_ap(name), ACT.Square, scale=0.5), name)

            def bn_relu(t, conv, h):
                name = f"cv_{t}_{conv}_{h}"
                wait_job(act, name)
                if t:
                    wait_job(act, f"bk_0_{conv}_1")
                for j in range(CG // 2):
                    cg = h * (CG // 2) + j
                    ins = copy(gT[conv][:, cg * 128:cg * 128 + 128], slot_ap(name)[:, j * 128:j * 128 + 128],
                               ACT.Relu, scale=bnp[:, 0, conv, cg:cg + 1], bias=bnp[:, 1, conv, cg:cg + 1])
                frees(ins, name)

            def to_natural(t, conv, h):
                name = f"bk_{t}_{conv}_{h}"
                wait_job(act, name)
                dst = (gN, g1N)[conv][t].rearrange("p (w a g) -> p w a g", a=CP, g=CG)
                src = slot_ap(name).rearrange("p (g a w) -> p w a g", a=CP, w=W)
                frees(copy(dst[:, :, :, h * (CG // 2):(h + 1) * (CG // 2)], src), name)

            def c14(t):
                wait_reader(act, f"gx_{t}_0")
                wait_reader(act, f"gx_{t}_1")
                copy(coef[:, t, 2, :], coef[:, t, 1, :], bias=1.0 + 2.0 * DT).then_inc(c14_ready, 1)

            def reciprocal_first(t):
                act.wait_ge(u_ready, t + 1)
                act.wait_ge(den_const, 1)
                then(copy(coef[:, t, 2, :], coef[:, t, 3, :], ACT.Ln, bias=minus16[:, 0:1]))
                copy(coef[:, t, 4, :], coef[:, t, 2, :], ACT.Exp, scale=-1.0).then_inc(y_ready, 1)
                act.wait_ge(y_ready, 2 * t + 1)
                copy(coef[:, t, 5, :], coef[:, t, 4, :], scale=-2.0 * DT).then_inc(y_ready, 1)

            def d_of(t):
                act.wait_ge(sb_ready, t + 1)
                copy(coef[:, t, 0, :], coef[:, t, 2, :], scale=-1.0, bias=1.0).then_inc(d_ready, 1)
                copy(coef[:, t, A0, :], coef[:, t, 2, :], scale=-2.0, bias=1.0).then_inc(d_ready, 1)

            nc.scalar.preload_act_table_set("natural_log_exp_and_others")
            for i, row in enumerate(bn_rows):
                act.dma_start(bn4[:, i // 2, (i % 2) * CG:(i % 2 + 1) * CG], row).then_inc(bn_in, 16)
            wait_job(act, "wtaps")
            frees(copy(taps[:, :], slot_ap("wtaps")[:, 0:2 * 9 * CG]), "wtaps")
            rsqrt_first(CP, 2 * CG)
            square_of(0)
            act.wait_ge(compact_ready, 1)
            act.wait_ge(zero_ready, 1)
            for conv in range(2):
                for q in range(CP):
                    p = slice(32 * q, 32 * q + 32)
                    m = slice(48 * conv, 48 * conv + 48)
                    copy(taps_m[p, m, 32 * q:32 * q + 32], compact[p, m, :]).then_inc(taps_m_ready, 1)
                if conv == 0:
                    rsqrt_first(128, GROUPS)
                    wait_job(act, "bnrow")
                    frees(copy(bnp[:, :, :, :].rearrange("p a b c -> p (a b c)"), slot_ap("bnrow")[:, 0:4 * CG]),
                          "bnrow")
            act.wait_ge(sobel_src, 2)
            for i, (m, scale) in enumerate(((smooth, 1.0), (smooth, -1.0), (diff, 1.0), (diff, 2.0))):
                copy(sobel_m[:, i, :], m[:, :, :].rearrange("p a b -> p (a b)"), scale=scale)\
                    .then_inc(sobel_m_ready, 1)
            reorder(0)
            split_hi(0)
            wrap(0, 0, s_halo)
            to_depthwise(0, 0)
            to_depthwise(0, 1)
            act.wait_ge(wl_in, 32)
            copy(wabs, wl, ACT.Abs, accum_out=wred[:, 0:1]).then_inc(wabs_ready, 1)
            act.wait_ge(vsum_ready, 1)
            square_of(1)
            for g in range(2):
                for h in range(2):
                    sobel_square(0, g, h)
            rsqrt_first(128, GROUPS)
            c14(0)
            wait_reader(act, "bnrow")
            bn_relu(0, 0, 0)
            reorder(1)
            split_hi(1)
            reciprocal_first(0)
            bn_relu(0, 0, 1)
            bn_relu(0, 1, 0)
            to_natural(0, 0, 0)
            bn_relu(0, 1, 1)
            to_natural(0, 0, 1)
            to_depthwise(1, 0)
            to_depthwise(1, 1)
            wrap(1, 0, s_halo)
            d_of(0)
            to_natural(0, 1, 0)
            to_natural(0, 1, 1)
            act.wait_ge(tern_ready, 1)
            act.wait_ge(zero_ready, 2)
            tern = wtern.rearrange("p (y x o) -> p y x o", y=3, x=3)
            for b, k, m, dx in ((0, 0, 0, 0), (0, 1, 0, 1), (0, 1, 1, 0), (1, 0, 0, 2), (1, 0, 1, 1), (1, 1, 1, 2)):
                copy(dense_m[64 * k:64 * k + 64, b, :, 64 * m:64 * m + 64], tern[64 * k:64 * k + 64, :, dx, :])\
                    .then_inc(dense_m_ready, 1)
            bn_relu(1, 0, 0)
            bn_relu(1, 0, 1)
            bn_relu(1, 1, 0)
            act.wait_ge(dense_m_ready, 6)
            to_natural(1, 0, 0)
            bn_relu(1, 1, 1)
            to_natural(1, 0, 1)
            to_natural(1, 1, 0)
            sobel_square(1, 0, 0)
            sobel_square(1, 0, 1)
            to_natural(1, 1, 1)
            sobel_square(1, 1, 0)
            sobel_square(1, 1, 1)
            c14(1)
            reciprocal_first(1)
            d_of(1)
            rsqrt_first(128, 1)

            def relu_bn_out(t, h):
                wait_job(act, f"th_{t}_{h}")
                frees(copy(half(coef[:, t, 0, :], h), slot_ap(f"th_{t}_{h}"), ACT.Relu, scale=outw[:, 2:3],
                           bias=outw[:, 3:4]), f"th_{t}_{h}")

            def normalise(t):
                act.wait_ge(norm_ready, t + 1)
                x1 = coef[:, t, 2, :].rearrange("p (j b h) -> p j b h", b=BT, h=H)
                xn = coef[:, t, 3, :].rearrange("p (j b h) -> p j b h", b=BT, h=H)
                for b in range(BT):
                    copy(xn[:, :, b, :], x1[:, :, b, :], ACT.Identity, scale=gn2[:, t, 3, b:b + 1],
                         bias=gn2[:, t, 4, b:b + 1]).then_inc(xn_ready, 1)
                act.wait_ge(xn_ready, BT * (t + 1))
                copy(coef[:, t, 5, :].bitcast(f32r), coef[:, t, 3, :]).then_inc(xh_ready, 1)

            def to_odd_pairs(t):
                if t:
                    wait_job(act, "cf_0_1")
                act.wait_ge(pads_ready, 2)
                act.wait_ge(xh_ready, t + 1)
                for dst, src in ((hi, coef[:, t, 5, :]), (lo, coef[:, t, 6, :])):
                    if dst is lo:
                        act.wait_ge(xl_ready, t + 1)
                    d = dst[:, :].rearrange("p (r h) -> p r h", h=HP)
                    s = src.rearrange("p (r h) -> p r h", h=H)
                    copy(d[0:64, BT:, 1:1 + H], s[64:128, :, :]).then_inc(odd_ready, 1)
                    copy(d[64:128, 0:PAIRS * BT, 1:1 + H], s[0:64, :, :]).then_inc(odd_ready, 1)

            def relu_dense(t, h):
                act.wait_ge(alpha_ready, 1)
                wait_job(act, f"cf_{t}_{h}")
                frees(copy(half(coef[:, t, 0, :], h), slot_ap(f"cf_{t}_{h}"), ACT.Relu, scale=wred[:, 7:8],
                           bias=outp[:, 4:5]), f"cf_{t}_{h}")

            def take_out(t, h):
                wait_job(act, f"tb_{t}_{h}")
                frees(copy(half(coef[:, t, 4, :], h), slot_ap(f"tb_{t}_{h}")), f"tb_{t}_{h}")

            for k in range(STEPS - 1):
                for t in range(TILES):
                    if k == 0:
                        act.wait_ge(product, products_through(0, t))
                        copy(h_at(t, 0), h_at(t, 0), scale=1.0 + DT).then_inc(s_scaled, 1)
                    wait_reader(act, f"acc_{k}_{t}_0")
                    wait_reader(act, f"acc_{k}_{t}_1")
                    wrap(t, k + 1, halo_ready)
            act.wait_ge(outw_ready, 1)
            for h in range(2):
                relu_bn_out(0, h)
            for h in range(2):
                relu_bn_out(1, h)
            rsqrt_first(128, BT)
            normalise(0)
            to_odd_pairs(0)
            rsqrt_first(128, BT)
            normalise(1)
            for h in range(2):
                relu_dense(0, h)
            to_odd_pairs(1)
            for h in range(2):
                take_out(0, h)
            for h in range(2):
                relu_dense(1, h)
            for h in range(2):
                take_out(1, h)

        @blk.vector
        def _(dve):
            steps, asked = [0], [0]
            V = nc.vector

            def then(ins):
                steps[0] += 1
                ins.then_inc(dve_step, 1)
                dve.wait_ge(dve_step, steps[0])

            def signal(ins, done, value):
                ins.then_inc(done, 1)
                dve.wait_ge(done, value)

            def stt(out_ap, in0, scalar, in1, op0, op1):
                return V.scalar_tensor_tensor(out=out_ap, in0=in0, scalar=scalar, in1=in1, op0=op0, op1=op1)

            def leave(name):
                frees(V.memset(wred[:, 6:7], 0.0), name)

            def rsqrt(p, n, dst, ask):
                asked[0] += 1
                signal(ask, rs_asked, asked[0])
                dve.wait_ge(rs_given, asked[0])
                y, v, a = rs_y[0:p, 0:n], rs_in[0:p, 0:n], rs_t[0:p, 0, 0:n]
                then(V.tensor_tensor(a, y, y, ALU.mult))
                then(V.tensor_tensor(a, a, v, ALU.mult))
                then(V.tensor_scalar(a, a, -0.5, 1.5, ALU.mult, ALU.add))
                then(V.tensor_tensor(dst, y, a, ALU.mult))

            def over_w(ap32):
                return ap32.unsqueeze(1).unsqueeze(3).broadcast_to([128, W, GROUPS, 2])

            def grouped(ap):
                return ap.rearrange("p w (g c) -> p w g c", c=2)

            def sum_x(t):
                dve.wait_ge(x_loaded[t], 16)
                V.tensor_reduce(gsum[:, t, 0, :], x_in[t].rearrange("p (w g c) -> p g w c", g=GROUPS, c=2),
                                AX.XY, ALU.add).then_inc(xsum_ready, 1)

            def centre(t):
                wait_job(dve, f"mean_{t}")
                ins = V.tensor_scalar(gsum[:, t, 1, :], slot_ap(f"mean_{t}")[:, 0:GROUPS], 1.0 / PER_GROUP, None,
                                      ALU.mult)
                frees(ins, f"mean_{t}")
                wait_reader(dve, f"mean_{t}")
                signal(V.tensor_tensor(grouped(h_at(t, 0)), grouped(wc(x_in[t])), over_w(gsum[:, t, 1, :]),
                                       ALU.subtract), xm_ready, t + 1)

            def sum_squares(t):
                dve.wait_ge(sq_ready, t + 1)
                signal(V.tensor_reduce(gsum[:, t, 2, :], square.rearrange("p (w g c) -> p g w c", g=GROUPS, c=2),
                                       AX.XY, ALU.add), vsum_ready, t + 1)

            def scale_s(t):
                wait_job(dve, f"var_{t}")
                ask = V.tensor_scalar(rs_in[:, :], slot_ap(f"var_{t}")[:, 0:GROUPS], 1.0 / PER_GROUP, GN1_EPS,
                                      ALU.mult, ALU.add)
                rsqrt(128, GROUPS, gsum[:, t, 3, :], ask)
                s = grouped(h_at(t, 0))
                leave(f"var_{t}")
                signal(V.tensor_tensor(s, s, over_w(gsum[:, t, 3, :]), ALU.mult), s_ready, t + 1)

            def split_lo(t):
                dve.wait_ge(s_hi, t + 1)
                if t:
                    wait_job(dve, "gx_0_1")
                signal(V.tensor_tensor(wc(lo[:, 0:N]), h_at(t, 0), wc(hi[:, 0:N].bitcast(f32)), ALU.subtract),
                       s_lo, t + 1)

            dve.wait_ge(near_ready, 3)
            then(V.tensor_reduce(tapmask[:, :, :], near[:, :, :, :].rearrange("p d a w -> p d w a"), AX.X, ALU.add))
            wait_reader(dve, "wtaps")
            m4 = compact.rearrange("p (k g) w -> p k g w", g=CG)
            tv = taps[:, :].rearrange("p (k x g) -> p k x g", x=3, g=CG)

            def tap(d):
                return tv[:, :, d, :].unsqueeze(3).broadcast_to([128, 6, CG, 32])

            def mask(d):
                return tapmask[:, d, :].unsqueeze(1).unsqueeze(1).broadcast_to([128, 6, CG, 32])

            then(V.tensor_tensor(m4, tap(1), mask(1), ALU.mult))
            then(V.copy_predicated(m4, mask(0).bitcast(i32), tap(0)))
            sum_x(0)
            signal(V.copy_predicated(m4, mask(2).bitcast(i32), tap(2)), compact_ready, 1)
            centre(0)

            dve.wait_ge(bn_in, 16 * 8)
            gamma, beta, mean = bn4[:, 0, :], bn4[:, 1, :], bn4[:, 2, :]
            rsqrt(CP, 2 * CG, bn4w[:, 0, :],
                  V.tensor_scalar(rs_in[0:CP, 0:2 * CG], bn4[:, 3, :], BN_EPS, None, ALU.add))
            then(V.tensor_tensor(bn4w[:, 1, :], bn4w[:, 0, :], gamma, ALU.mult))
            then(V.tensor_tensor(bn4w[:, 2, :], bn4w[:, 1, :], mean, ALU.mult))
            then(V.tensor_tensor(bn4w[:, 2, :], beta, bn4w[:, 2, :], ALU.subtract))
            signal(V.tensor_scalar(bn4o[:, :, :], bn4w[:, 1:3, :], DT, None, ALU.mult), bn4_ready, 1)

            sum_squares(0)
            sum_x(1)
            scale_s(0)
            centre(1)
            split_lo(0)
            sum_squares(1)

            wait_job(dve, "wsum")
            ins = V.tensor_scalar(wred[:, 1:2], slot_ap("wsum")[:, 0:1], 1.0 / (2 * 9 * C * C), 0.7, ALU.mult,
                                  ALU.mult)
            frees(ins, "wsum")
            wait_reader(dve, "wsum")
            then(V.tensor_scalar(wred[:, 2:3], wred[:, 1:2], -1.0, None, ALU.mult))
            then(V.tensor_scalar(wtern, wabs, wred[:, 1:2], None, ALU.is_gt))
            then(V.tensor_reduce(wred[:, 4:5], wtern, AX.X, ALU.add))
            then(V.tensor_tensor(wtern, wtern, wabs, ALU.mult))
            signal(V.tensor_reduce(wred[:, 3:4], wtern, AX.X, ALU.add), kept_ready, 1)
            then(V.tensor_scalar(wabs, wl, wred[:, 1:2], None, ALU.is_ge))
            then(V.tensor_scalar(wl, wl, wred[:, 2:3], None, ALU.is_le))
            signal(V.tensor_tensor(wtern, wabs, wl, ALU.subtract), tern_ready, 1)

            scale_s(1)

            def coefficients(t):
                c = [coef[:, t, i, :] for i in range(NCOEF)]
                s = h_at(t, 0)
                dve.wait_ge(c14_ready, t + 1)
                signal(stt(c[3], c[0], 1.0 + 2 * DT, c[2], ALU.add, ALU.mult), u_ready, t + 1)
                if t == 0:
                    split_lo(1)
                dve.wait_ge(y_ready, 2 * t + 1)
                then(stt(c[2], c[3], -(2 * DT) ** 2, c[4], ALU.add, ALU.mult))
                dve.wait_ge(y_ready, 2 * t + 2)
                then(stt(c[3], c[2], -2.0, c[5], ALU.add, ALU.mult))
                then(stt(c[4], c[1], 1.0, c[3], ALU.add, ALU.mult))
                then(stt(c[5], c[0], 1.0, c[3], ALU.add, ALU.mult))
                signal(V.tensor_tensor(c[2], c[4], c[5], ALU.add), sb_ready, t + 1)
                for h in range(2):
                    wait_reader(dve, f"bk_{t}_0_{h}")
                    wait_reader(dve, f"bk_{t}_1_{h}")
                g, g1, e, e1 = wc(gN[t]), wc(g1N[t]), wc(c[3]), wc(scratch)
                V.tensor_tensor(e[:, 1:W - 1, :], g[:, 0:W - 2, :], g[:, 2:W, :], ALU.subtract)
                V.tensor_tensor(e[:, 0, :], g[:, W - 1, :], g[:, 1, :], ALU.subtract)
                then(V.tensor_tensor(e[:, W - 1, :], g[:, W - 2, :], g[:, 0, :], ALU.subtract))
                V.tensor_tensor(e1[:, :, 1:C - 1], g1[:, :, 0:C - 2], g1[:, :, 2:C], ALU.subtract)
                V.tensor_tensor(e1[:, :, 0:1], g1[:, :, C - 1:C], g1[:, :, 1:2], ALU.subtract)
                then(V.tensor_tensor(e1[:, :, C - 1:C], g1[:, :, C - 2:C - 1], g1[:, :, 0:1], ALU.subtract))
                then(V.tensor_tensor(c[3], c[3], scratch, ALU.add))
                dve.wait_ge(d_ready, 2 * t + 2)
                then(stt(c[AE], c[3], -1.0, c[0], ALU.mult, ALU.mult))
                then(stt(scratch, c[A0], 1.0 + DT, c[AE], ALU.mult, ALU.add))
                then(V.tensor_tensor(g1N[t], g1N[t], c[0], ALU.mult))
                then(V.tensor_tensor(c[AYM], c[5], g1N[t], ALU.subtract))
                then(V.tensor_tensor(c[AYP], c[5], g1N[t], ALU.add))
                then(stt(h_at(t, 1), wc(scratch), DT, s, ALU.add, ALU.mult))
                then(V.tensor_tensor(c[6], c[6], c[0], ALU.mult))
                then(stt(wc(c[FS]), wc(c[0]), 2 * DT, s, ALU.mult, ALU.mult))
                then(V.tensor_tensor(c[AXP], c[4], c[6], ALU.add))
                signal(stt(c[AXM], c[6], -2.0, c[AXP], ALU.mult, ALU.add), coef_ready, t + 1)

            coefficients(0)
            wait_job(dve, "alpha")
            then(V.reciprocal(wred[:, 5:6], slot_ap("alpha")[:, 1:2]))
            ins = V.tensor_tensor(wred[:, 7:8], slot_ap("alpha")[:, 0:1], wred[:, 5:6], ALU.mult)
            ins.then_inc(alpha_ready, 1)
            dve.wait_ge(alpha_ready, 1)
            leave("alpha")
            coefficients(1)

            dve.wait_ge(outp_in, 16 * 10)
            rsqrt(128, 1, outw[:, 0:1], V.tensor_scalar(rs_in[:, 0:1], outp[:, 3:4], BN_EPS, None, ALU.add))
            then(V.tensor_tensor(outw[:, 2:3], outw[:, 0:1], outp[:, 0:1], ALU.mult))
            then(V.tensor_tensor(outw[:, 1:2], outw[:, 2:3], outp[:, 2:3], ALU.mult))
            signal(V.tensor_tensor(outw[:, 3:4], outp[:, 1:2], outw[:, 1:2], ALU.subtract), outw_ready, 1)

            made = [0]
            sum_ends = {products_through(k, t): (k, t) for k in range(STEPS) for t in range(TILES)}

            def wait_summed(n):
                if n in sum_ends:
                    k, t = sum_ends[n]
                    wait_job(dve, f"acc_{k}_{t}_1")
                else:
                    dve.wait_ge(ring_free, n - sum(end < n for end in sum_ends))

            def multiply(t, k, a, dw, dc):
                slot = made[0] % RING
                if made[0] >= RING:
                    wait_summed(made[0] - RING + 1)
                made[0] += 1
                signal(V.tensor_tensor(wc(ring[:, slot, :]), wc(coef[:, t, a, :]), h_at(t, k, dw, dc), ALU.mult),
                       product, made[0])

            def rest(t, k):
                old = h_at(t, k + 1)
                if k == 1:
                    dve.wait_ge(s_scaled, t + 1)
                    then(stt(old, wc(coef[:, t, A0, :]), DT / (1.0 + DT), old, ALU.add, ALU.mult))
                elif k > 1:
                    then(V.tensor_tensor(old, old, wc(coef[:, t, A0, :]), ALU.mult))
                    then(V.tensor_tensor(old, old, wc(coef[:, t, FS, :]), ALU.add))

            def total(t, k):
                for h in range(2):
                    name = f"acc_{k}_{t}_{h}"
                    wait_job(dve, name)
                    old = h_at(t, k + 1, w0=h * W // 2, w1=(h + 1) * W // 2)
                    new = old if k < STEPS - 1 else wc(half(coef[:, t, 3, :], h))
                    frees(V.tensor_tensor(new, wc(slot_ap(name)), old, ALU.add), name)
                    wait_reader(dve, name)

            def residual(t):
                for h in range(2):
                    wait_reader(dve, f"th_{t}_{h}")
                    wait_job(dve, f"tx_{t}_{h}")
                    frees(V.tensor_tensor(half(coef[:, t, 2, :], h), slot_ap(f"tx_{t}_{h}"),
                                          half(coef[:, t, 0, :], h), ALU.add), f"tx_{t}_{h}")
                    wait_reader(dve, f"tx_{t}_{h}")
                x1 = coef[:, t, 2, :].rearrange("p (j b h) -> p j b h", b=BT, h=H)
                for b in range(BT):
                    ins = V.bn_stats(stats[:, b, :], x1[:, :, b, :])
                then(ins)
                for b in range(BT):
                    ins = V.bn_aggr(mv[:, t, b, :], stats[:, b, :])
                signal(ins, mv_ready, t + 1)

            def spread(t):
                wait_job(dve, f"mean2_{t}")
                frees(V.tensor_copy(gn2[:, t, 0, :], slot_ap(f"mean2_{t}")[:, 0:BT]), f"mean2_{t}")
                wait_reader(dve, f"mean2_{t}")
                then(V.tensor_tensor(gn2[:, t, 1, :], mv[:, t, :, 0], gn2[:, t, 0, :], ALU.subtract))
                then(V.tensor_tensor(gn2[:, t, 1, :], gn2[:, t, 1, :], gn2[:, t, 1, :], ALU.mult))
                signal(V.tensor_tensor(gn2[:, t, 2, :], mv[:, t, :, 1], gn2[:, t, 1, :], ALU.add), q_ready, t + 1)

            def second_norm(t):
                wait_job(dve, f"var2_{t}")
                rsqrt(128, BT, gn2[:, t, 3, :],
                      V.tensor_scalar(rs_in[:, 0:BT], slot_ap(f"var2_{t}")[:, 0:BT], GN2_EPS, None, ALU.add))
                leave(f"var2_{t}")
                signal(stt(gn2[:, t, 4, :], gn2[:, t, 0, :], -1.0, gn2[:, t, 3, :], ALU.mult, ALU.mult),
                       norm_ready, t + 1)

            def lower_half(t):
                dve.wait_ge(xh_ready, t + 1)
                signal(V.tensor_tensor(coef[:, t, 6, :], coef[:, t, 3, :], coef[:, t, 5, :], ALU.subtract),
                       xl_ready, t + 1)

            def output_sum(t):
                for h in range(2):
                    wait_reader(dve, f"cf_{t}_{h}")
                    signal(V.tensor_tensor(half(coef[:, t, 3, :], h), half(coef[:, t, 0, :], h),
                                           half(coef[:, t, 2, :], h), ALU.add), sum_ready, 2 * t + h + 1)

            before = None
            for k in range(STEPS):
                terms = [(AYM, 0, -1), (AYP, 0, 1), (AXM, -1, 0), (AXP, 1, 0)] + [(AE, 0, 0)] * (k > 0)
                for t in range(TILES):
                    if k == 0:
                        dve.wait_ge(s_halo, 4 * (t + 1))
                    else:
                        dve.wait_ge(halo_ready, 4 * (TILES * (k - 1) + t + 1))
                    rest(t, k)
                    for i, (a, dw, dc) in enumerate(terms):
                        multiply(t, k, a, dw, dc)
                        if i == 0 and before:
                            total(*before)
                    before = (t, k)
            residual(0)
            total(*before)
            spread(0)
            residual(1)
            second_norm(0)
            spread(1)
            lower_half(0)
            second_norm(1)
            lower_half(1)
            output_sum(0)
            output_sum(1)

        @blk.tensor
        def _(pe):
            mm = nc.tensor.matmul

            def take(name):
                if uses_before[name]:
                    pe.wait_ge(slot_free[slot_of[name]], uses_before[name])
                return slot_ap(name)

            def small(name, n, lhsT, rhs):
                mm(take(name)[:, 0:n], lhsT, rhs, start=True, stop=True).then_inc(pe_job, 1)

            def turns(name, blocks):
                dst = take(name)
                for j, src in enumerate(blocks):
                    ins = nc.tensor.transpose(dst[:, j * 128:j * 128 + 128], src, ident[:, :])
                ins.then_inc(pe_job, 1)

            def to_depthwise(t, h):
                pe.wait_ge(s_reordered, t + 1)
                turns(f"t2_{t}_{h}", [half(sT[t], h)[:, j * 128:j * 128 + 128] for j in range(CG // 2)])

            def sobel(t, g, h):
                pe.wait_ge(s_lo, t + 1)
                name = f"{('gy', 'gx')[g]}_{t}_{h}"
                dst = take(name)
                taps_w = ((0, 3), (1, 2), (-1, 2)) if g == 0 else ((1, 0), (-1, 1))
                for bank in range(2):
                    w0 = (2 * h + bank) * (BANK // C)
                    pieces = []
                    for dw, m in taps_w:
                        lo_w, hi_w = w0 + dw, w0 + BANK // C + dw
                        if lo_w < 0:
                            pieces += [(1, 0, 7, m), (0, 1, 1, m)]
                        elif hi_w > W:
                            pieces += [(0, lo_w, 7, m), (7, W - 2, 1, m)]
                        else:
                            pieces.append((0, lo_w, 8, m))
                    if pieces[0][2] < 8:
                        pieces.sort(key=lambda piece: -piece[2])
                    last = len(pieces) - 1
                    for i, (to, frm, count, m) in enumerate(pieces):
                        for part in (hi, lo):
                            ins = mm(dst[:, bank * BANK + to * C:bank * BANK + (to + count) * C],
                                     sobel_m[:, m, :], part[:, frm * C:(frm + count) * C],
                                     start=(i == 0 and part is hi), stop=(i == last and part is lo),
                                     skip_group_check=True)
                ins.then_inc(pe_job, 1)

            def depthwise(t, conv, h):
                name = f"cv_{t}_{conv}_{h}"
                pe.wait_ge(taps_m_ready, CP * (conv + 1))
                wait_reader(pe, f"t2_{t}_0")
                wait_reader(pe, f"t2_{t}_1")
                dst = take(name)
                for j in range(CG // 2):
                    cg = h * (CG // 2) + j
                    src = sT[t][:, cg * 128:cg * 128 + 128].rearrange("p (b h) -> p b h", h=H)
                    to = dst[:, j * 128:j * 128 + 128].rearrange("p (b h) -> p b h", h=H)
                    for dy, o, i in ((1, slice(0, H), slice(0, H)), (0, slice(1, H), slice(0, H - 1)),
                                     (2, slice(0, H - 1), slice(1, H))):
                        ins = mm(to[:, :, o], taps_m[:, 48 * conv + 16 * dy + cg, :], src[:, :, i],
                                 start=(dy == 1), stop=(dy == 2))
                ins.then_inc(pe_job, 1)

            def back(t, conv, h):
                wait_reader(pe, f"cv_{t}_{conv}_{h}")
                turns(f"bk_{t}_{conv}_{h}",
                      [gT[conv][:, cg * 128:cg * 128 + 128] for cg in range(h * (CG // 2), (h + 1) * (CG // 2))])

            summed = [0]

            def sum_products(t, k):
                dst = [take(f"acc_{k}_{t}_{h}") for h in range(2)]
                count = products_of(k)
                for i in range(count):
                    pe.wait_ge(product, summed[0] + 1)
                    src = ring[:, summed[0] % RING, :]
                    summed[0] += 1
                    for q in range(4):
                        ins = mm(dst[q // 2][:, (q % 2) * BANK:(q % 2 + 1) * BANK], ident[:, :],
                                 src[:, q * BANK:(q + 1) * BANK], start=(i == 0), stop=(i == count - 1))
                        if i == count - 1 and q == 1:
                            ins.then_inc(pe_job, 1)
                    if i < count - 1:
                        ins.then_inc(ring_free, 1)
                ins.then_inc(pe_job, 1)

            def paired(t, name, src, h):
                turns(f"{name}_{t}_{h}", [src[:, 2 * j:2 * j + 2, :] for j in range(h * 8, h * 8 + 8)])

            def h_paired(t):
                for h in range(2):
                    wait_reader(pe, f"acc_{STEPS - 1}_{t}_{h}")
                    paired(t, "th", wc(coef[:, t, 3, :]), h)

            def x_paired(t):
                pe.wait_ge(x_again[t], 16)
                for h in range(2):
                    paired(t, "tx", wc(coef[:, t, 1, :]), h)

            def group_mean2(t):
                pe.wait_ge(mv_ready, t + 1)
                small(f"mean2_{t}", BT, pairavg[:, :, :, :].rearrange("p a b c -> p (a b c)"), mv[:, t, :, 0])

            def group_var2(t):
                pe.wait_ge(q_ready, t + 1)
                small(f"var2_{t}", BT, pairavg[:, :, :, :].rearrange("p a b c -> p (a b c)"), gn2[:, t, 2, :])

            def dense(t):
                pe.wait_ge(odd_ready, 4 * (t + 1))
                for h in range(2):
                    dst = take(f"cf_{t}_{h}")
                    for bank in range(2):
                        j0 = 4 * (2 * h + bank)
                        to = dst[:, bank * BANK:(bank + 1) * BANK].rearrange("p (r h) -> p r h", h=H)
                        steps = [(b, dy, part) for b in range(2) for dy in range(3) for part in (hi, lo)]
                        for i, (b, dy, part) in enumerate(steps):
                            rows = part[:, :].rearrange("p (r h) -> p r h", h=HP)
                            ins = mm(to, dense_m[:, b, dy, :], rows[:, (j0 + b) * BT:(j0 + b + 4) * BT, dy:dy + H],
                                     start=(i == 0), stop=(i == len(steps) - 1))
                    ins.then_inc(pe_job, 1)

            def out_natural(t):
                for h in range(2):
                    pe.wait_ge(sum_ready, 2 * t + h + 1)
                    turns(f"tb_{t}_{h}", [half(coef[:, t, 3, :], h)[:, j * 128:j * 128 + 128] for j in range(8)])

            blockm = block[:, :, :].rearrange("p a b -> p (a b)")
            spreadm = spread4[:, :, :].rearrange("p a b -> p (a b)")
            pe.wait_ge(spread_ready, 1)
            pe.wait_ge(taps_in, 32)
            small("wtaps", 2 * 9 * CG, spreadm, taps4[:, :, :, :].rearrange("p a k g -> p (a k g)"))
            pe.wait_ge(near_ready, 1)
            pe.wait_ge(xsum_ready, 1)
            small("mean_0", GROUPS, blockm, gsum[:, 0, 0, :])
            pe.wait_ge(bn4_ready, 1)
            small("bnrow", 4 * CG, spreadm, bn4o[:, :, :].rearrange("p a g -> p (a g)"))
            pe.wait_ge(vsum_ready, 1)
            small("var_0", GROUPS, blockm, gsum[:, 0, 2, :])
            pe.wait_ge(xsum_ready, 2)
            small("mean_1", GROUPS, blockm, gsum[:, 1, 0, :])
            pe.wait_ge(ident_ready, 1)
            to_depthwise(0, 0)
            to_depthwise(0, 1)
            pe.wait_ge(sobel_m_ready, 4)
            for g in range(2):
                for h in range(2):
                    sobel(0, g, h)
            pe.wait_ge(ones_ready, 1)
            pe.wait_ge(wabs_ready, 1)
            small("wsum", 1, ones[:, :], wred[:, 0:1])
            pe.wait_ge(vsum_ready, 2)
            small("var_1", GROUPS, blockm, gsum[:, 1, 2, :])
            depthwise(0, 0, 0)
            depthwise(0, 0, 1)
            depthwise(0, 1, 0)
            back(0, 0, 0)
            depthwise(0, 1, 1)
            back(0, 0, 1)
            to_depthwise(1, 0)
            to_depthwise(1, 1)
            back(0, 1, 0)
            back(0, 1, 1)
            pe.wait_ge(kept_ready, 1)
            small("alpha", 2, ones[:, :], wred[:, 3:5])
            depthwise(1, 0, 0)
            depthwise(1, 0, 1)
            depthwise(1, 1, 0)
            back(1, 0, 0)
            depthwise(1, 1, 1)
            back(1, 0, 1)
            back(1, 1, 0)
            sobel(1, 0, 0)
            sobel(1, 0, 1)
            back(1, 1, 1)
            sobel(1, 1, 0)
            sobel(1, 1, 1)
            for k in range(STEPS):
                for t in range(TILES):
                    if (k, t) == (STEPS - 1, 1):
                        h_paired(0)
                        x_paired(0)
                    sum_products(t, k)
            pe.wait_ge(pairavg_ready, 2)
            group_mean2(0)
            h_paired(1)
            x_paired(1)
            group_var2(0)
            group_mean2(1)
            pe.wait_ge(dense_m_ready, 6)
            dense(0)
            group_var2(1)
            out_natural(0)
            dense(1)
            out_natural(1)
    return nc


_NAMES = ["x", "L0_conv_wg", "L0_conv_wg1", "L0_conv_g_gamma", "L0_conv_g1_gamma", "L0_conv_g_beta", "L0_conv_g1_beta",
          "L0_conv_g_mean", "L0_conv_g1_mean", "L0_conv_g_var", "L0_conv_g1_var", "L0_conv_out_gamma",
          "L0_conv_out_beta", "L0_conv_out_mean", "L0_conv_out_var", "L1_conv_b", "L1_conv_W"]


def kernel(**inputs):
    import numpy as _np
    import concourse.bacc as _bacc
    from concourse import mybir as _mybir
    from concourse.bass_utils import run_bass_kernel_spmd as _run

    nc = _bacc.Bacc("TRN2", target_bir_lowering=False, num_devices=1)
    arrays, ap = {}, {}
    for name in _NAMES:
        a = _np.ascontiguousarray(inputs[name])
        arrays[f"in_{name}"] = a
        ap[name] = nc.dram_tensor(f"in_{name}", a.shape, _mybir.dt.from_np(a.dtype), kind="ExternalInput").ap()
    out = nc.dram_tensor("out", (B, H, W, C), _mybir.dt.float32, kind="ExternalOutput").ap()
    bn_rows = [ap[n].rearrange("(a g) -> a g", g=CG) for n in _NAMES[3:11]]
    out_cols = [ap[n].rearrange("(c o) -> c o", o=1) for n in _NAMES[11:16]]
    network(nc, ap["x"], ap["L0_conv_wg"], ap["L0_conv_wg1"], bn_rows, out_cols, ap["L1_conv_W"], out)
    r = _run(nc, [arrays], core_ids=[0])
    return r.results[0]["out"]
```

```python
from contextlib import ExitStack

from concourse import mybir

B, H, W, C = 8, 32, 32, 64
TILES = 2
BT = B // TILES
N = W * C
HALF = N // 2
BANK = 512
CP = 4
CG = C // CP
PITCH = C + 2
ROWS = W + 2
STEPS = 5
DT = 0.2
BN_EPS, GN1_EPS, GN2_EPS = 1e-3, 1e-5, 1e-5
GROUPS = 32
PER_GROUP = H * W * (C // GROUPS)
PAIRS = W // 2
HP = H + 2
NCOEF = 7
A0, AE, FS, AXM, AXP, AYM, AYP = 1, 3, 0, 6, 4, 2, 5
RING = 3
SLOTS = 4
ORDER = [(0, 0), (1, 0), (0, 1), (2, 0), (1, 1), (3, 0), (2, 1), (4, 0), (3, 1), (4, 1)]
S = 1.0 / (2.0 * DT)
FAR = 200



def job_table():
    early = ["wtaps", "mean_0", "bnrow", "var_0", "mean_1", "t2_0_0", "t2_0_1",
             "gy_0_0", "gy_0_1", "gx_0_0", "gx_0_1", "cv_0_0_0", "var_1", "cv_0_0_1",
             "cv_0_1_0", "bk_0_0_0", "cv_0_1_1", "bk_0_0_1", "bk_0_1_0", "bk_0_1_1", "wsum", "t2_1_0", "t2_1_1",
             "alpha",
             "cv_1_0_0", "cv_1_0_1", "gy_1_0", "gy_1_1", "gx_1_0", "gx_1_1",
             "cv_1_1_0", "bk_1_0_0", "cv_1_1_1", "bk_1_0_1", "bk_1_1_0", "bk_1_1_1"]
    jobs = [(name, i % SLOTS) for i, name in enumerate(early)]

    def halves(name, t):
        return [(f"{name}_{t}_{h}", 2 * t + h) for h in range(2)]

    for k, t in ORDER:
        if (k, t) == (STEPS - 2, 1):
            jobs += halves("th", 0) + halves("tx", 0)
        if (k, t) == (STEPS - 1, 1):
            jobs += [("mean2_0", 0), ("var2_0", 1)]
        jobs += [(f"acc_{k}_{t}_{h}", 2 * t + h) for h in range(2)]
    jobs += [("cf_0_0", 0)] + halves("th", 1) + halves("tx", 1) + [("cf_0_1", 1)]
    jobs += [("mean2_1", 2), ("var2_1", 3)] + halves("tb", 0) + halves("cf", 1) + halves("tb", 1)
    return jobs


def network(nc, x, wg, wg1, bn_rows, out_cols, conv_w, out):
    f32, f32r, i32 = mybir.dt.float32, mybir.dt.float32r, mybir.dt.int32
    ALU, ACT, AX = mybir.AluOpType, mybir.ActivationFunctionType, mybir.AxisListType

    jobs = job_table()
    job_no = {name: i for i, (name, _) in enumerate(jobs)}
    slot_of = dict(jobs)
    uses_before, seen = {}, [0] * SLOTS
    for name, slot in jobs:
        uses_before[name] = seen[slot]
        seen[slot] += 1

    with ExitStack() as ctx:
        def sb(name, shape, dt=f32):
            return ctx.enter_context(nc.sbuf_tensor(name, shape, dt))

        def sem(name):
            return ctx.enter_context(nc.semaphore(name))

        coef = sb("coef", [128, TILES, NCOEF, N])
        state = sb("state", [128, TILES, 2, ROWS, PITCH])
        ring = sb("ring", [128, RING, N])
        hi = sb("hi", [128, (PAIRS + 1) * BT * HP], f32r)
        lo = sb("lo", [128, (PAIRS + 1) * BT * HP], f32r)
        sobel_m = sb("sobel_m", [128, 4, 128], f32r)
        dense_m = sb("dense_m", [128, 2, 3, 128], f32r)
        ident = sb("ident", [128, 128])
        block = sb("block", [128, CP, 32])
        smooth = sb("smooth", [128, CP, 32])
        diff = sb("diff", [128, CP, 32])
        near = sb("near", [128, 3, CP, 32])
        tapmask = sb("tapmask", [128, 3, 32])
        spread4 = sb("spread4", [CP, CP, 32])
        pairavg = sb("pairavg", [128, 2, GROUPS, 2])
        ones = sb("ones", [128, 128])
        taps4 = sb("taps4", [CP, 2, 9, CG])
        taps = sb("taps", [128, 2 * 9 * CG])
        bn4 = sb("bn4", [CP, 4, 2 * CG])
        bn4w = sb("bn4w", [CP, 3, 2 * CG])
        bn4o = sb("bn4o", [CP, 2, 2 * CG])
        bnp = sb("bnp", [128, 2, 2, CG])
        outp = sb("outp", [128, 5])
        outw = sb("outw", [128, 4])
        gsum = sb("gsum", [128, TILES, 4, GROUPS])
        rs_in = sb("rs_in", [128, GROUPS])
        rs_ln = sb("rs_ln", [128, GROUPS])
        rs_y = sb("rs_y", [128, GROUPS])
        rs_t = sb("rs_t", [128, 3, GROUPS])
        wred = sb("wred", [128, 8])
        stats = sb("stats", [128, BT, 6])
        mv = sb("mv", [128, TILES, BT, 2])
        minus1 = sb("minus1", [128, 1])
        gn2 = sb("gn2", [128, TILES, 6, BT])
        psum = ctx.enter_context(nc.psum_tensor("psum", [128, SLOTS, HALF], f32))

        x_in = [ring[:, t, :] for t in range(TILES)]
        square = ring[:, 2, :]
        compact = coef[:, 0, 5:7, :].rearrange("p a n -> p (a n)")[:, 0:96 * 32].rearrange("p (m w) -> p m w", w=32)
        taps_m = coef[:, 1, 0:6, :].rearrange("p a n -> p (a n)").rearrange("p (m n) -> p m n", n=128)
        wl = coef[:, 1, 6, 0:9 * C]
        wabs = coef[:, 1, 6, 9 * C:18 * C]
        wtern = coef[:, 1, 6, 18 * C:27 * C]
        sT = [state[:, t, 1, :, :].rearrange("p r q -> p (r q)")[:, 0:N] for t in range(TILES)]
        gT = [ring[:, 0, :], ring[:, 1, :]]
        gN = [coef[:, t, 6, :] for t in range(TILES)]
        g1N = sT

        def h_at(t, k, dw=0, dc=0, w0=0, w1=W):
            return state[:, t, k % 2, 1 + dw + w0:1 + dw + w1, 1 + dc:1 + dc + C]

        def wc(ap):
            return ap.rearrange("p (w c) -> p w c", c=C)

        def half(ap, h):
            return ap[:, h * HALF:(h + 1) * HALF]

        def expansion(conv, q):
            p, m = slice(32 * q, 32 * q + 32), slice(48 * conv, 48 * conv + 48)
            return taps_m[p, m, 32 * q:32 * q + 32], compact[p, m, :]

        def slot_ap(name):
            return psum[:, slot_of[name], :]

        taps_in, bn_in, outp_in, wl_in = sem("taps_in"), sem("bn_in"), sem("outp_in"), sem("wl_in")
        x_loaded = [sem("x_loaded0"), sem("x_loaded1")]
        x_again = [sem("x_again0"), sem("x_again1")]
        out_stored = sem("out_stored")
        pe_job = sem("pe_job")
        slot_free = [sem(f"slot_free{q}") for q in range(SLOTS)]
        pool_step, dve_step, act_step = sem("pool_step"), sem("dve_step"), sem("act_step")
        spread_ready, near_ready, ident_ready, sobel_src = (sem(n) for n in (
            "spread_ready", "near_ready", "ident_ready", "sobel_src"))
        ones_ready, pairavg_ready, zero_ready = sem("ones_ready"), sem("pairavg_ready"), sem("zero_ready")
        compact_ready, taps_m_ready, taps_m_too = sem("compact_ready"), sem("taps_m_ready"), sem("taps_m_too")
        xsum_ready, xm_ready, sq_ready, vsum_ready = (sem(n) for n in (
            "xsum_ready", "xm_ready", "sq_ready", "vsum_ready"))
        s_ready, s_hi, s_lo, s_halo = sem("s_ready"), sem("s_hi"), sem("s_lo"), sem("s_halo")
        s_reordered, den_const = sem("s_reordered"), sem("den_const")
        rs_asked, rs_given = sem("rs_asked"), sem("rs_given")
        bn4_ready, outw_ready = sem("bn4_ready"), sem("outw_ready")
        sobel_m_ready, dense_m_ready = sem("sobel_m_ready"), sem("dense_m_ready")
        c14_ready, u_ready, y_ready, sb_ready, d_ready, coef_ready = (sem(n) for n in (
            "c14_ready", "u_ready", "y_ready", "sb_ready", "d_ready", "coef_ready"))
        product, ring_free = sem("product"), sem("ring_free")
        halo_ready, s_scaled = sem("halo_ready"), sem("s_scaled")
        wabs_ready, kept_ready, alpha_ready, tern_ready = (sem(n) for n in (
            "wabs_ready", "kept_ready", "alpha_ready", "tern_ready"))
        mv_ready, q_ready, norm_ready, xn_ready, xh_ready, xl_ready = (sem(n) for n in (
            "mv_ready", "q_ready", "norm_ready", "xn_ready", "xh_ready", "xl_ready"))
        pads_ready, odd_ready, sum_ready = sem("pads_ready"), sem("odd_ready"), sem("sum_ready")

        def wait_job(eng, name):
            eng.wait_ge(pe_job, job_no[name] + 1)

        def wait_reader(eng, name):
            eng.wait_ge(slot_free[slot_of[name]], uses_before[name] + 1)

        def frees(ins, name):
            ins.then_inc(slot_free[slot_of[name]], 1)

        def products_of(k):
            return 4 if k == 0 else 5

        def products_through(k, t):
            return sum(products_of(kk) for kk, _ in ORDER[:ORDER.index((k, t)) + 1])

        def states_through(k, t):
            return sum(kk < STEPS - 1 for kk, _ in ORDER[:ORDER.index((k, t)) + 1])

        x_nat = x.rearrange("(t b) h w c -> t (b h) (w c)", t=TILES)
        out_nat = out.rearrange("(t b) h w c -> t (b h) (w c)", t=TILES)

        blk = ctx.enter_context(nc.Block())

        @blk.sync
        def _(sp):
            sp.dma_start(x_in[0], x_nat[0]).then_inc(x_loaded[0], 16)
            for conv, src in enumerate((wg, wg1)):
                sp.dma_start(taps4[:, conv, :, :],
                             src.rearrange("y x (a g) -> a (y x) g", g=CG)).then_inc(taps_in, 16)
            sp.dma_start(x_in[1], x_nat[1]).then_inc(x_loaded[1], 16)
            sp.wait_ge(x_loaded[1], 16)
            for k in range(2):
                sp.dma_start(wl[64 * k:64 * k + 64, :].rearrange("i (k o) -> i k o", o=C),
                             conv_w.rearrange("y x i o -> i (y x) o")).then_inc(wl_in, 16)
            for i, col in enumerate(out_cols):
                for k in range(2):
                    sp.dma_start(outp[64 * k:64 * k + 64, i:i + 1], col).then_inc(outp_in, 16)
            for t in range(TILES):
                sp.wait_ge(product, products_through(STEPS - 1, t) - products_of(STEPS - 1) + 1)
                sp.dma_start(coef[:, t, 1, :], x_nat[t]).then_inc(x_again[t], 16)
            for t in range(TILES):
                for h in range(2):
                    wait_reader(sp, f"tb_{t}_{h}")
                    sp.dma_start(half(out_nat[t], h), half(coef[:, t, 4, :], h)).then_inc(out_stored, 16)
            sp.wait_ge(out_stored, 16 * 2 * TILES)

        @blk.gpsimd
        def _(pool):
            steps = [0]

            def then(ins):
                steps[0] += 1
                ins.then_inc(pool_step, 1)
                pool.wait_ge(pool_step, steps[0])

            def select(ap, pattern, base, mult, fill, op=ALU.not_equal):
                return nc.gpsimd.affine_select(out=ap, in_=ap, pattern=pattern, compare_op=op, fill=fill, base=base,
                                               channel_multiplier=mult)

            def times_block(ap):
                return nc.gpsimd.tensor_tensor(ap, ap, block[:, :, :], ALU.mult)

            nc.gpsimd.memset(minus1[:, :], -1.0).then_inc(den_const, 1)
            then(nc.gpsimd.memset(spread4[:, :, :], 0.0))
            select(spread4[:, :, :], [[-1, CP], [0, 32]], 0, 1, 1.0).then_inc(spread_ready, 1)
            then(nc.gpsimd.memset(block[:, :, :], 1.0))
            then(select(block[:, :, :], [[-32, CP], [0, 32]], 0, 1, 0.0, ALU.is_ge))
            then(select(block[:, :, :], [[32, CP], [0, 32]], 31, -1, 0.0, ALU.is_ge))
            then(nc.gpsimd.memset(near[:, :, :, :], 0.0))
            for d in range(3):
                then(select(near[:, d, :, :], [[-32, CP], [-1, 32]], 1 - d, 1, 1.0))
                times_block(near[:, d, :, :]).then_inc(near_ready, 1)
            then(nc.gpsimd.memset(ident[:, :], 0.0))
            select(ident[:, :], [[-1, 128]], 0, 1, 1.0).then_inc(ident_ready, 1)
            then(nc.gpsimd.memset(smooth[:, :, :], 0.0))
            then(select(smooth[:, :, :], [[-32, CP], [-1, 32]], 0, 1, 2.0))
            then(select(smooth[:, :, :], [[-32, CP], [-1, 32]], -1, 1, 1.0))
            then(select(smooth[:, :, :], [[-32, CP], [-1, 32]], 1, 1, 1.0))
            then(times_block(smooth[:, :, :]))
            then(select(smooth[:, :, :], [[-32, CP], [FAR, 32]], -1, 1, 2.0))
            select(smooth[:, :, :], [[-32, CP], [FAR, 32]], -30 - 31 * FAR, 1, 2.0).then_inc(sobel_src, 1)
            then(nc.gpsimd.memset(diff[:, :, :], 0.0))
            then(select(diff[:, :, :], [[-32, CP], [-1, 32]], -1, 1, 1.0))
            then(select(diff[:, :, :], [[-32, CP], [-1, 32]], 1, 1, -1.0))
            then(times_block(diff[:, :, :]))
            then(select(diff[:, :, :], [[0, CP], [1, 32]], 0, 0, 0.0, ALU.is_gt))
            select(diff[:, :, :], [[0, CP], [-1, 32]], 31, 0, 0.0, ALU.is_gt).then_inc(sobel_src, 1)
            nc.gpsimd.memset(ones[:, :], 1.0).then_inc(ones_ready, 1)
            for conv in range(2):
                nc.gpsimd.memset(coef[:, 1, 3 * conv:3 * conv + 3, :].rearrange("p a n -> p (a n)"), 0.0)\
                    .then_inc(zero_ready, 1)
            nc.gpsimd.memset(dense_m[:, :, :, :].bitcast(f32), 0.0).then_inc(zero_ready, 1)
            then(nc.gpsimd.memset(pairavg[:, :, :, :], 0.25))
            for k in range(2):
                part = pairavg[64 * k:64 * k + 64, :, :, :]
                then(select(part, [[0, 2], [-2, GROUPS], [0, 2]], 0, 1, 0.0, ALU.is_ge))
                select(part, [[0, 2], [2, GROUPS], [0, 2]], 1, -1, 0.0, ALU.is_ge).then_inc(pairavg_ready, 1)
                pool.wait_ge(pairavg_ready, k + 1)
            wait_job(pool, "gx_1_1")
            nc.gpsimd.memset(hi[:, :].bitcast(f32), 0.0).then_inc(pads_ready, 1)
            nc.gpsimd.memset(lo[:, :].bitcast(f32), 0.0).then_inc(pads_ready, 1)

        @blk.scalar
        def _(act):
            steps, asked = [0], [0]

            def then(ins):
                steps[0] += 1
                ins.then_inc(act_step, 1)
                act.wait_ge(act_step, steps[0])

            def copy(dst, src, func=ACT.Copy, **kw):
                return nc.scalar.activation(dst, src, func, **kw)

            def rsqrt_first(p, n):
                asked[0] += 1
                act.wait_ge(rs_asked, asked[0])
                then(copy(rs_ln[0:p, 0:n], rs_in[0:p, 0:n], ACT.Ln))
                copy(rs_y[0:p, 0:n], rs_ln[0:p, 0:n], ACT.Exp, scale=-0.5).then_inc(rs_given, 1)

            def square_of(t):
                act.wait_ge(xm_ready, t + 1)
                copy(wc(square), h_at(t, 0), ACT.Square).then_inc(sq_ready, 1)

            def wrap(t, k, done):
                s = state[:, t, k % 2, :, :]
                copy(s[:, 0, 1:1 + C], s[:, W, 1:1 + C]).then_inc(done, 1)
                copy(s[:, W + 1, 1:1 + C], s[:, 1, 1:1 + C]).then_inc(done, 1)
                copy(s[:, 1:1 + W, 0:1], s[:, 1:1 + W, C:C + 1]).then_inc(done, 1)
                copy(s[:, 1:1 + W, C + 1:C + 2], s[:, 1:1 + W, 1:2]).then_inc(done, 1)

            def split_hi(t):
                act.wait_ge(s_ready, t + 1)
                wait_job(act, "gx_0_1")
                copy(wc(hi[:, 0:N]), h_at(t, 0)).then_inc(s_hi, 1)

            def reorder(t):
                act.wait_ge(s_ready, t + 1)
                copy(sT[t].rearrange("p (g a w) -> p g a w", a=CP, w=W),
                     h_at(t, 0).rearrange("p w (a g) -> p g a w", g=CG)).then_inc(s_reordered, 1)

            def to_depthwise(t, h):
                wait_job(act, f"t2_{t}_1")
                frees(copy(half(sT[t], h), slot_ap(f"t2_{t}_{h}")), f"t2_{t}_{h}")

            def sobel_square(t, g, h):
                name = f"{('gy', 'gx')[g]}_{t}_{h}"
                wait_job(act, name)
                frees(copy(half(coef[:, t, g, :], h), slot_ap(name), ACT.Square, scale=0.5 * S ** 0.5), name)

            def bn_bias(t, conv, h):
                name = f"cv_{t}_{conv}_{h}"
                wait_job(act, name)
                wait_job(act, f"bk_0_{conv}_1")
                for j in range(CG // 2):
                    cg = h * (CG // 2) + j
                    ins = copy(gT[conv][:, cg * 128:cg * 128 + 128], slot_ap(name)[:, j * 128:j * 128 + 128],
                               ACT.Identity, bias=bnp[:, 1, conv, cg:cg + 1])
                frees(ins, name)

            def to_natural(t, conv, h):
                name = f"bk_{t}_{conv}_{h}"
                wait_job(act, name)
                dst = (gN, g1N)[conv][t].rearrange("p (w a g) -> p w a g", a=CP, g=CG)
                src = slot_ap(name).rearrange("p (g a w) -> p w a g", a=CP, w=W)
                frees(copy(dst[:, :, :, h * (CG // 2):(h + 1) * (CG // 2)], src, ACT.Relu), name)

            def reciprocal_first(t):
                act.wait_ge(u_ready, t + 1)
                act.wait_ge(den_const, 1)
                then(copy(coef[:, t, 2, :], coef[:, t, 3, :], ACT.Ln, bias=minus1[:, 0:1]))
                copy(coef[:, t, 4, :], coef[:, t, 2, :], ACT.Exp, scale=-1.0).then_inc(y_ready, 1)

            def d_of(t):
                act.wait_ge(sb_ready, t + 1)
                copy(coef[:, t, 0, :], coef[:, t, 2, :], bias=1.0).then_inc(d_ready, 1)
                copy(coef[:, t, A0, :], coef[:, t, 2, :], scale=2.0, bias=1.0).then_inc(d_ready, 1)

            nc.scalar.preload_act_table_set("natural_log_exp_and_others")
            for i, row in enumerate(bn_rows):
                act.dma_start(bn4[:, i // 2, (i % 2) * CG:(i % 2 + 1) * CG], row).then_inc(bn_in, 16)
            wait_job(act, "wtaps")
            frees(copy(taps[:, :], slot_ap("wtaps")[:, 0:2 * 9 * CG]), "wtaps")
            rsqrt_first(CP, 2 * CG)
            square_of(0)
            wait_job(act, "bnrow")
            frees(copy(bnp[:, :, :, :].rearrange("p a b c -> p (a b c)"), slot_ap("bnrow")[:, 0:4 * CG]), "bnrow")
            act.wait_ge(sobel_src, 2)
            for i, (m, scale) in enumerate(((smooth, 1.0), (smooth, -1.0), (diff, 1.0), (diff, 2.0))):
                copy(sobel_m[:, i, :], m[:, :, :].rearrange("p a b -> p (a b)"), scale=scale)\
                    .then_inc(sobel_m_ready, 1)
            rsqrt_first(128, GROUPS)
            reorder(0)
            to_depthwise(0, 0)
            to_depthwise(0, 1)

            def expand(conv):
                act.wait_ge(compact_ready, 1)
                act.wait_ge(zero_ready, conv + 1)
                for q in range(2):
                    copy(*expansion(conv, q)).then_inc(taps_m_ready, 1)

            sobel_square(0, 0, 0)
            sobel_square(0, 0, 1)
            expand(0)
            sobel_square(0, 1, 0)
            sobel_square(0, 1, 1)
            square_of(1)
            expand(1)
            rsqrt_first(128, GROUPS)
            reciprocal_first(0)
            split_hi(1)
            reorder(1)
            act.wait_ge(wl_in, 32)
            copy(wabs, wl, ACT.Abs, accum_out=wred[:, 0:1]).then_inc(wabs_ready, 1)
            wrap(0, 0, s_halo)
            to_natural(0, 0, 0)
            to_natural(0, 0, 1)
            to_natural(0, 1, 0)
            to_natural(0, 1, 1)
            to_depthwise(1, 0)
            to_depthwise(1, 1)
            d_of(0)
            wrap(1, 0, s_halo)
            bn_bias(1, 0, 0)
            bn_bias(1, 0, 1)
            for g in range(2):
                for h in range(2):
                    sobel_square(1, g, h)
            rsqrt_first(128, 1)
            act.wait_ge(tern_ready, 1)
            act.wait_ge(zero_ready, 3)
            tern = wtern.rearrange("p (y x o) -> p y x o", y=3, x=3)
            for b, k, m, dx in ((0, 0, 0, 0), (0, 1, 0, 1), (0, 1, 1, 0), (1, 0, 0, 2), (1, 0, 1, 1), (1, 1, 1, 2)):
                copy(dense_m[64 * k:64 * k + 64, b, :, 64 * m:64 * m + 64], tern[64 * k:64 * k + 64, :, dx, :])\
                    .then_inc(dense_m_ready, 1)
            bn_bias(1, 1, 0)
            act.wait_ge(dense_m_ready, 6)
            to_natural(1, 0, 0)
            bn_bias(1, 1, 1)
            reciprocal_first(1)
            to_natural(1, 0, 1)
            to_natural(1, 1, 0)
            to_natural(1, 1, 1)
            d_of(1)

            def relu_bn_out(t, h):
                wait_job(act, f"th_{t}_{h}")
                frees(copy(half(coef[:, t, 0, :], h), slot_ap(f"th_{t}_{h}"), ACT.Relu, scale=outw[:, 2:3],
                           bias=outw[:, 3:4]), f"th_{t}_{h}")

            def normalise(t):
                act.wait_ge(norm_ready, t + 1)
                x1 = coef[:, t, 2, :].rearrange("p (j b h) -> p j b h", b=BT, h=H)
                xn = coef[:, t, 3, :].rearrange("p (j b h) -> p j b h", b=BT, h=H)
                for b in range(BT):
                    copy(xn[:, :, b, :], x1[:, :, b, :], ACT.Identity, scale=gn2[:, t, 3, b:b + 1],
                         bias=gn2[:, t, 4, b:b + 1]).then_inc(xn_ready, 1)
                act.wait_ge(xn_ready, BT * (t + 1))
                copy(coef[:, t, 5, :].bitcast(f32r), coef[:, t, 3, :]).then_inc(xh_ready, 1)

            def to_odd_pairs(t):
                if t:
                    wait_job(act, "cf_0_1")
                act.wait_ge(pads_ready, 2)
                act.wait_ge(xh_ready, t + 1)
                for dst, src in ((hi, coef[:, t, 5, :]), (lo, coef[:, t, 6, :])):
                    if dst is lo:
                        act.wait_ge(xl_ready, t + 1)
                    d = dst[:, :].rearrange("p (r h) -> p r h", h=HP)
                    s = src.rearrange("p (r h) -> p r h", h=H)
                    copy(d[0:64, BT:, 1:1 + H], s[64:128, :, :]).then_inc(odd_ready, 1)
                    copy(d[64:128, 0:PAIRS * BT, 1:1 + H], s[0:64, :, :]).then_inc(odd_ready, 1)

            def relu_dense(t, h):
                act.wait_ge(alpha_ready, 1)
                wait_job(act, f"cf_{t}_{h}")
                frees(copy(half(coef[:, t, 0, :], h), slot_ap(f"cf_{t}_{h}"), ACT.Relu, scale=wred[:, 7:8],
                           bias=outp[:, 4:5]), f"cf_{t}_{h}")

            def take_out(t, h):
                wait_job(act, f"tb_{t}_{h}")
                frees(copy(half(coef[:, t, 4, :], h), slot_ap(f"tb_{t}_{h}")), f"tb_{t}_{h}")

            for k, t in ORDER[:-1]:
                if k == 0:
                    act.wait_ge(product, products_through(0, t))
                    copy(h_at(t, 0), h_at(t, 0), scale=1.0 + DT).then_inc(s_scaled, 1)
                if k < STEPS - 1:
                    if k == STEPS - 2 and t == 1:
                        act.wait_ge(outw_ready, 1)
                        relu_bn_out(0, 0)
                        relu_bn_out(0, 1)
                    wait_reader(act, f"acc_{k}_{t}_0")
                    wait_reader(act, f"acc_{k}_{t}_1")
                    wrap(t, k + 1, halo_ready)
            rsqrt_first(128, BT)
            normalise(0)
            to_odd_pairs(0)
            relu_dense(0, 0)
            relu_bn_out(1, 0)
            relu_bn_out(1, 1)
            relu_dense(0, 1)
            rsqrt_first(128, BT)
            normalise(1)
            take_out(0, 0)
            take_out(0, 1)
            to_odd_pairs(1)
            relu_dense(1, 0)
            relu_dense(1, 1)
            take_out(1, 0)
            take_out(1, 1)

        @blk.vector
        def _(dve):
            steps, asked = [0], [0]
            V = nc.vector

            def then(ins):
                steps[0] += 1
                ins.then_inc(dve_step, 1)
                dve.wait_ge(dve_step, steps[0])

            def signal(ins, done, value):
                ins.then_inc(done, 1)
                dve.wait_ge(done, value)

            def stt(out_ap, in0, scalar, in1, op0, op1):
                return V.scalar_tensor_tensor(out=out_ap, in0=in0, scalar=scalar, in1=in1, op0=op0, op1=op1)

            def leave(name):
                frees(V.memset(wred[:, 6:7], 0.0), name)

            def ask_rsqrt(ask):
                asked[0] += 1
                signal(ask, rs_asked, asked[0])

            def rsqrt(p, n, dst, ask=None):
                if ask is not None:
                    ask_rsqrt(ask)
                dve.wait_ge(rs_given, asked[0])
                y, v, a = rs_y[0:p, 0:n], rs_in[0:p, 0:n], rs_t[0:p, 0, 0:n]
                then(V.tensor_tensor(a, y, y, ALU.mult))
                then(V.tensor_tensor(a, a, v, ALU.mult))
                then(V.tensor_scalar(a, a, -0.5, 1.5, ALU.mult, ALU.add))
                then(V.tensor_tensor(dst, y, a, ALU.mult))

            def over_w(ap32):
                return ap32.unsqueeze(1).unsqueeze(3).broadcast_to([128, W, GROUPS, 2])

            def grouped(ap):
                return ap.rearrange("p w (g c) -> p w g c", c=2)

            def sum_x(t):
                dve.wait_ge(x_loaded[t], 16)
                V.tensor_reduce(gsum[:, t, 0, :], x_in[t].rearrange("p (w g c) -> p g w c", g=GROUPS, c=2),
                                AX.XY, ALU.add).then_inc(xsum_ready, 1)

            def mean_of(t):
                wait_job(dve, f"mean_{t}")
                frees(V.tensor_scalar(gsum[:, t, 1, :], slot_ap(f"mean_{t}")[:, 0:GROUPS], 1.0 / PER_GROUP, None,
                                      ALU.mult), f"mean_{t}")

            def centre(t):
                wait_reader(dve, f"mean_{t}")
                signal(V.tensor_tensor(grouped(h_at(t, 0)), grouped(wc(x_in[t])), over_w(gsum[:, t, 1, :]),
                                       ALU.subtract), xm_ready, t + 1)

            def sum_squares(t):
                dve.wait_ge(sq_ready, t + 1)
                signal(V.tensor_reduce(gsum[:, t, 2, :], square.rearrange("p (w g c) -> p g w c", g=GROUPS, c=2),
                                       AX.XY, ALU.add), vsum_ready, t + 1)

            def scale_s(t):
                wait_job(dve, f"var_{t}")
                ask = V.tensor_scalar(rs_in[:, :], slot_ap(f"var_{t}")[:, 0:GROUPS], 1.0 / PER_GROUP, GN1_EPS,
                                      ALU.mult, ALU.add)
                rsqrt(128, GROUPS, gsum[:, t, 3, :], ask)
                s = grouped(h_at(t, 0))
                leave(f"var_{t}")
                signal(V.tensor_tensor(s, s, over_w(gsum[:, t, 3, :]), ALU.mult), s_ready, t + 1)

            def split_lo(t):
                dve.wait_ge(s_hi, t + 1)
                signal(V.tensor_tensor(wc(lo[:, 0:N]), h_at(t, 0), wc(hi[:, 0:N].bitcast(f32)), ALU.subtract),
                       s_lo, t + 1)

            sum_x(0)
            dve.wait_ge(near_ready, 3)
            then(V.tensor_reduce(tapmask[:, :, :], near[:, :, :, :].rearrange("p d a w -> p d w a"), AX.X, ALU.add))

            dve.wait_ge(bn_in, 16 * 8)
            gamma, beta, mean = bn4[:, 0, :], bn4[:, 1, :], bn4[:, 2, :]
            ask_rsqrt(V.tensor_scalar(rs_in[0:CP, 0:2 * CG], bn4[:, 3, :], BN_EPS, None, ALU.add))
            mean_of(0)
            centre(0)
            rsqrt(CP, 2 * CG, bn4w[:, 0, :])
            then(V.tensor_tensor(bn4w[:, 1, :], bn4w[:, 0, :], gamma, ALU.mult))
            then(V.tensor_tensor(bn4w[:, 2, :], bn4w[:, 1, :], mean, ALU.mult))
            then(V.tensor_tensor(bn4w[:, 2, :], beta, bn4w[:, 2, :], ALU.subtract))
            signal(V.tensor_scalar(bn4o[:, :, :], bn4w[:, 1:3, :], DT, None, ALU.mult), bn4_ready, 1)

            sum_squares(0)
            sum_x(1)
            scale_s(0)
            mean_of(1)
            signal(V.tensor_copy(wc(hi[:, 0:N]), h_at(0, 0)), s_hi, 1)
            split_lo(0)

            wait_reader(dve, "wtaps")
            wait_reader(dve, "bnrow")
            tv2 = taps[:, :].rearrange("p (v k g) -> p v k g", v=2, g=CG)
            then(V.tensor_tensor(tv2, tv2, bnp[:, 0, :, :].unsqueeze(2).broadcast_to([128, 2, 9, CG]), ALU.mult))
            m4 = compact.rearrange("p (k g) w -> p k g w", g=CG)
            tv = taps[:, :].rearrange("p (k x g) -> p k x g", x=3, g=CG)

            def tap(d):
                return tv[:, :, d, :].unsqueeze(3).broadcast_to([128, 6, CG, 32])

            def mask(d):
                return tapmask[:, d, :].unsqueeze(1).unsqueeze(1).broadcast_to([128, 6, CG, 32])

            then(V.tensor_tensor(m4, tap(1), mask(1), ALU.mult))
            then(V.copy_predicated(m4, mask(0).bitcast(i32), tap(0)))
            signal(V.copy_predicated(m4, mask(2).bitcast(i32), tap(2)), compact_ready, 1)

            def expand(conv):
                dve.wait_ge(zero_ready, conv + 1)
                for q in range(2, CP):
                    V.tensor_copy(*expansion(conv, q)).then_inc(taps_m_too, 1)

            expand(0)
            centre(1)
            expand(1)
            sum_squares(1)

            def ternary():
                wait_job(dve, "wsum")
                ins = V.tensor_scalar(wred[:, 1:2], slot_ap("wsum")[:, 0:1], 1.0 / (2 * 9 * C * C), 0.7, ALU.mult,
                                      ALU.mult)
                frees(ins, "wsum")
                wait_reader(dve, "wsum")
                then(V.tensor_scalar(wred[:, 2:3], wred[:, 1:2], -1.0, None, ALU.mult))
                then(V.tensor_scalar(wtern, wabs, wred[:, 1:2], None, ALU.is_gt))
                then(V.tensor_reduce(wred[:, 4:5], wtern, AX.X, ALU.add))
                then(V.tensor_tensor(wtern, wtern, wabs, ALU.mult))
                signal(V.tensor_reduce(wred[:, 3:4], wtern, AX.X, ALU.add), kept_ready, 1)
                then(V.tensor_scalar(wabs, wl, wred[:, 1:2], None, ALU.is_ge))
                then(V.tensor_scalar(wl, wl, wred[:, 2:3], None, ALU.is_le))
                signal(V.tensor_tensor(wtern, wabs, wl, ALU.subtract), tern_ready, 1)


            def denominator(t):
                for h in range(2):
                    wait_reader(dve, f"gy_{t}_{h}")
                    wait_reader(dve, f"gx_{t}_{h}")
                then(V.tensor_scalar(coef[:, t, 2, :], coef[:, t, 1, :], (1.0 + 2 * DT) * S, None, ALU.add))
                if t:
                    wait_job(dve, "cv_1_1_1")
                signal(stt(coef[:, t, 3, :], coef[:, t, 0, :], (1.0 + 2 * DT) * S, coef[:, t, 2, :], ALU.add,
                           ALU.mult), u_ready, t + 1)

            def newton(t):
                c = [coef[:, t, i, :] for i in range(NCOEF)]
                dve.wait_ge(y_ready, t + 1)
                then(stt(c[2], c[3], -1.0, c[4], ALU.add, ALU.mult))
                then(stt(c[3], c[2], -2.0, c[4], ALU.add, ALU.mult))

            def diffusivities(t, before_sum=lambda: None):
                c = [coef[:, t, i, :] for i in range(NCOEF)]
                then(stt(c[4], c[1], S, c[3], ALU.add, ALU.mult))
                if t == 0:
                    dve.wait_ge(taps_m_ready, 4)
                then(stt(c[5], c[0], S, c[3], ALU.add, ALU.mult))
                before_sum()
                signal(V.tensor_tensor(c[2], c[4], c[5], ALU.add), sb_ready, t + 1)

            def divergence(t):
                for h in range(2):
                    wait_reader(dve, f"bk_{t}_0_{h}")
                    wait_reader(dve, f"bk_{t}_1_{h}")
                g, g1, e, e1 = wc(gN[t]), wc(g1N[t]), wc(coef[:, t, 3, :]), wc(coef[:, t, 2, :])
                V.tensor_tensor(e[:, 1:W - 1, :], g[:, 0:W - 2, :], g[:, 2:W, :], ALU.subtract)
                V.tensor_tensor(e[:, 0, :], g[:, W - 1, :], g[:, 1, :], ALU.subtract)
                then(V.tensor_tensor(e[:, W - 1, :], g[:, W - 2, :], g[:, 0, :], ALU.subtract))
                dve.wait_ge(d_ready, 2 * t + 2)
                V.tensor_tensor(e1[:, :, 1:C - 1], g1[:, :, 0:C - 2], g1[:, :, 2:C], ALU.subtract)
                V.tensor_tensor(e1[:, :, 0:1], g1[:, :, C - 1:C], g1[:, :, 1:2], ALU.subtract)
                then(V.tensor_tensor(e1[:, :, C - 1:C], g1[:, :, C - 2:C - 1], g1[:, :, 0:1], ALU.subtract))
                then(V.tensor_tensor(coef[:, t, 3, :], coef[:, t, 3, :], coef[:, t, 2, :], ALU.add))

            def over_channels(t):
                c = [coef[:, t, i, :] for i in range(NCOEF)]
                then(stt(c[AE], c[3], -1.0, c[0], ALU.mult, ALU.mult))
                then(V.tensor_tensor(g1N[t], g1N[t], c[0], ALU.mult))
                then(stt(c[AYM], c[5], -1.0, g1N[t], ALU.mult, ALU.subtract))
                then(V.tensor_tensor(c[AYP], g1N[t], c[5], ALU.subtract))
                then(V.tensor_tensor(c[6], c[6], c[0], ALU.mult))

            def first_centre(t):
                c = [coef[:, t, i, :] for i in range(NCOEF)]
                s = h_at(t, 0)
                then(stt(h_at(t, 1), wc(c[AE]), -1.0, s, ALU.add, ALU.mult))
                then(stt(wc(c[FS]), wc(c[0]), 2 * DT, s, ALU.mult, ALU.mult))
                then(stt(h_at(t, 1), wc(c[FS]), (2.0 + 2 * DT) / (2 * DT), h_at(t, 1), ALU.mult, ALU.add))

            def over_columns(t):
                c = [coef[:, t, i, :] for i in range(NCOEF)]
                then(V.tensor_tensor(c[AXP], c[6], c[4], ALU.subtract))
                then(stt(c[AXM], c[6], -2.0, c[AXP], ALU.mult, ALU.add))

            made = [0]
            sum_ends = {products_through(k, t): (k, t) for k in range(STEPS) for t in range(TILES)}

            def wait_summed(n):
                if n in sum_ends:
                    k, t = sum_ends[n]
                    wait_job(dve, f"acc_{k}_{t}_1")
                else:
                    dve.wait_ge(ring_free, n - sum(end < n for end in sum_ends))

            def multiply(t, k, a, dw, dc):
                slot = made[0] % RING
                if (k, t) == ORDER[0]:
                    wait_job(dve, "bk_1_1_1")
                if made[0] >= RING:
                    wait_summed(made[0] - RING + 1)
                made[0] += 1
                signal(V.tensor_tensor(wc(ring[:, slot, :]), wc(coef[:, t, a, :]), h_at(t, k, dw, dc), ALU.mult),
                       product, made[0])

            def rest(t, k):
                old = h_at(t, k + 1)
                if k == 1:
                    dve.wait_ge(s_scaled, t + 1)
                    then(stt(old, wc(coef[:, t, A0, :]), DT / (1.0 + DT), old, ALU.add, ALU.mult))
                elif k > 1:
                    then(V.tensor_tensor(old, old, wc(coef[:, t, A0, :]), ALU.mult))
                    then(V.tensor_tensor(old, old, wc(coef[:, t, FS, :]), ALU.add))

            def total(t, k):
                for h in range(2):
                    name = f"acc_{k}_{t}_{h}"
                    wait_job(dve, name)
                    old = h_at(t, k + 1, w0=h * W // 2, w1=(h + 1) * W // 2)
                    new = old if k < STEPS - 1 else wc(half(coef[:, t, 3, :], h))
                    frees(V.tensor_tensor(new, wc(slot_ap(name)), old, ALU.add), name)
                    wait_reader(dve, name)

            def residual(t):
                for h in range(2):
                    wait_reader(dve, f"th_{t}_{h}")
                    wait_job(dve, f"tx_{t}_{h}")
                    frees(V.tensor_tensor(half(coef[:, t, 2, :], h), slot_ap(f"tx_{t}_{h}"),
                                          half(coef[:, t, 0, :], h), ALU.add), f"tx_{t}_{h}")
                    wait_reader(dve, f"tx_{t}_{h}")
                x1 = coef[:, t, 2, :].rearrange("p (j b h) -> p j b h", b=BT, h=H)
                for b in range(BT):
                    ins = V.bn_stats(stats[:, b, :], x1[:, :, b, :])
                then(ins)
                for b in range(BT):
                    ins = V.bn_aggr(mv[:, t, b, :], stats[:, b, :])
                signal(ins, mv_ready, t + 1)

            def spread(t):
                wait_job(dve, f"mean2_{t}")
                frees(V.tensor_copy(gn2[:, t, 0, :], slot_ap(f"mean2_{t}")[:, 0:BT]), f"mean2_{t}")
                wait_reader(dve, f"mean2_{t}")
                then(V.tensor_tensor(gn2[:, t, 1, :], mv[:, t, :, 0], gn2[:, t, 0, :], ALU.subtract))
                then(V.tensor_tensor(gn2[:, t, 1, :], gn2[:, t, 1, :], gn2[:, t, 1, :], ALU.mult))
                signal(V.tensor_tensor(gn2[:, t, 2, :], mv[:, t, :, 1], gn2[:, t, 1, :], ALU.add), q_ready, t + 1)

            def second_norm(t):
                wait_job(dve, f"var2_{t}")
                rsqrt(128, BT, gn2[:, t, 3, :],
                      V.tensor_scalar(rs_in[:, 0:BT], slot_ap(f"var2_{t}")[:, 0:BT], GN2_EPS, None, ALU.add))
                leave(f"var2_{t}")
                signal(stt(gn2[:, t, 4, :], gn2[:, t, 0, :], -1.0, gn2[:, t, 3, :], ALU.mult, ALU.mult),
                       norm_ready, t + 1)

            def lower_half(t):
                dve.wait_ge(xh_ready, t + 1)
                signal(V.tensor_tensor(coef[:, t, 6, :], coef[:, t, 3, :], coef[:, t, 5, :], ALU.subtract),
                       xl_ready, t + 1)

            def output_sum(t):
                for h in range(2):
                    wait_reader(dve, f"cf_{t}_{h}")
                    signal(V.tensor_tensor(half(coef[:, t, 3, :], h), half(coef[:, t, 0, :], h),
                                           half(coef[:, t, 2, :], h), ALU.add), sum_ready, 2 * t + h + 1)

            def step(k, t, before=None, then_do=()):
                if k == 0:
                    dve.wait_ge(s_halo, 4 * (t + 1))
                else:
                    dve.wait_ge(halo_ready, 4 * states_through(k - 1, t))
                rest(t, k)
                terms = [(AYM, 0, -1), (AYP, 0, 1), (AXM, -1, 0), (AXP, 1, 0)] + [(AE, 0, 0)] * (k > 0)
                for i, (a, dw, dc) in enumerate(terms):
                    multiply(t, k, a, dw, dc)
                    if i == 0 and before:
                        total(*before)
                    for at, what in then_do:
                        if at == i:
                            what()

            def bn_bias(t, conv, h):
                name = f"cv_{t}_{conv}_{h}"
                wait_job(dve, name)
                groups = slice(h * (CG // 2), (h + 1) * (CG // 2))
                frees(V.tensor_tensor(half(gT[conv], h).rearrange("p (g r) -> p g r", g=CG // 2),
                                      slot_ap(name).rearrange("p (g r) -> p g r", g=CG // 2),
                                      bnp[:, 1, conv, groups].unsqueeze(2).broadcast_to([128, CG // 2, BT * H]),
                                      ALU.add), name)

            denominator(0)
            scale_s(1)
            bn_bias(0, 0, 0)
            newton(0)
            bn_bias(0, 0, 1)
            split_lo(1)
            bn_bias(0, 1, 0)
            diffusivities(0, lambda: bn_bias(0, 1, 1))
            ternary()
            divergence(0)
            wait_job(dve, "alpha")
            then(V.reciprocal(wred[:, 5:6], slot_ap("alpha")[:, 1:2]))
            ins = V.tensor_tensor(wred[:, 7:8], slot_ap("alpha")[:, 0:1], wred[:, 5:6], ALU.mult)
            ins.then_inc(alpha_ready, 1)
            dve.wait_ge(alpha_ready, 1)
            leave("alpha")
            over_channels(0)
            first_centre(0)

            dve.wait_ge(outp_in, 16 * 10)
            rsqrt(128, 1, outw[:, 0:1], V.tensor_scalar(rs_in[:, 0:1], outp[:, 3:4], BN_EPS, None, ALU.add))
            then(V.tensor_tensor(outw[:, 2:3], outw[:, 0:1], outp[:, 0:1], ALU.mult))
            then(V.tensor_tensor(outw[:, 1:2], outw[:, 2:3], outp[:, 2:3], ALU.mult))
            signal(V.tensor_tensor(outw[:, 3:4], outp[:, 1:2], outw[:, 1:2], ALU.subtract), outw_ready, 1)

            denominator(1)
            over_columns(0)
            newton(1)
            diffusivities(1)
            step(0, 0)
            divergence(1)
            total(0, 0)
            over_channels(1)
            step(1, 0)
            first_centre(1)
            total(0, 1)
            over_columns(1)
            step(0, 1)
            before = (1, 0)
            for k, t in ORDER[3:-1]:
                step(k, t, before)
                before = (t, k)
            residual(0)
            total(*before)
            spread(0)
            step(STEPS - 1, 1, None, ((0, lambda: second_norm(0)), (3, lambda: lower_half(0))))
            total(1, STEPS - 1)
            residual(1)
            output_sum(0)
            spread(1)
            second_norm(1)
            lower_half(1)
            output_sum(1)

        @blk.tensor
        def _(pe):
            mm = nc.tensor.matmul

            def take(name):
                if uses_before[name]:
                    pe.wait_ge(slot_free[slot_of[name]], uses_before[name])
                return slot_ap(name)

            def small(name, n, lhsT, rhs):
                mm(take(name)[:, 0:n], lhsT, rhs, start=True, stop=True).then_inc(pe_job, 1)

            def turns(name, blocks):
                dst = take(name)
                for j, src in enumerate(blocks):
                    ins = nc.tensor.transpose(dst[:, j * 128:j * 128 + 128], src, ident[:, :])
                ins.then_inc(pe_job, 1)

            def to_depthwise(t, h):
                pe.wait_ge(s_reordered, t + 1)
                turns(f"t2_{t}_{h}", [half(sT[t], h)[:, j * 128:j * 128 + 128] for j in range(CG // 2)])

            def sobel(t, g, h):
                pe.wait_ge(s_lo, t + 1)
                name = f"{('gy', 'gx')[g]}_{t}_{h}"
                dst = take(name)
                taps_w = ((0, 3), (1, 2), (-1, 2)) if g == 0 else ((1, 0), (-1, 1))
                for bank in range(2):
                    w0 = (2 * h + bank) * (BANK // C)
                    pieces = []
                    for dw, m in taps_w:
                        lo_w, hi_w = w0 + dw, w0 + BANK // C + dw
                        if lo_w < 0:
                            pieces += [(1, 0, 7, m), (0, 1, 1, m)]
                        elif hi_w > W:
                            pieces += [(0, lo_w, 7, m), (7, W - 2, 1, m)]
                        else:
                            pieces.append((0, lo_w, 8, m))
                    if pieces[0][2] < 8:
                        pieces.sort(key=lambda piece: -piece[2])
                    last = len(pieces) - 1
                    for i, (to, frm, count, m) in enumerate(pieces):
                        for part in (hi, lo):
                            ins = mm(dst[:, bank * BANK + to * C:bank * BANK + (to + count) * C],
                                     sobel_m[:, m, :], part[:, frm * C:(frm + count) * C],
                                     start=(i == 0 and part is hi), stop=(i == last and part is lo),
                                     skip_group_check=True)
                ins.then_inc(pe_job, 1)

            def depthwise(t, conv, h):
                name = f"cv_{t}_{conv}_{h}"
                pe.wait_ge(taps_m_ready, 2 * (conv + 1))
                pe.wait_ge(taps_m_too, 2 * (conv + 1))
                wait_reader(pe, f"t2_{t}_0")
                wait_reader(pe, f"t2_{t}_1")
                dst = take(name)
                for j in range(CG // 2):
                    cg = h * (CG // 2) + j
                    src = sT[t][:, cg * 128:cg * 128 + 128].rearrange("p (b h) -> p b h", h=H)
                    to = dst[:, j * 128:j * 128 + 128].rearrange("p (b h) -> p b h", h=H)
                    for dy, o, i in ((1, slice(0, H), slice(0, H)), (0, slice(1, H), slice(0, H - 1)),
                                     (2, slice(0, H - 1), slice(1, H))):
                        ins = mm(to[:, :, o], taps_m[:, 48 * conv + 16 * dy + cg, :], src[:, :, i],
                                 start=(dy == 1), stop=(dy == 2))
                ins.then_inc(pe_job, 1)

            def back(t, conv, h):
                wait_reader(pe, f"cv_{t}_{conv}_{h}")
                turns(f"bk_{t}_{conv}_{h}",
                      [gT[conv][:, cg * 128:cg * 128 + 128] for cg in range(h * (CG // 2), (h + 1) * (CG // 2))])

            summed = [0]

            def sum_products(t, k, between=()):
                dst = [take(f"acc_{k}_{t}_{h}") for h in range(2)]
                count = products_of(k)
                for i in range(count):
                    pe.wait_ge(product, summed[0] + 1)
                    src = ring[:, summed[0] % RING, :]
                    summed[0] += 1
                    for q in range(4):
                        ins = mm(dst[q // 2][:, (q % 2) * BANK:(q % 2 + 1) * BANK], ident[:, :],
                                 src[:, q * BANK:(q + 1) * BANK], start=(i == 0), stop=(i == count - 1))
                        if i == count - 1 and q == 1:
                            ins.then_inc(pe_job, 1)
                    if i < count - 1:
                        ins.then_inc(ring_free, 1)
                    for at, what in between:
                        if at == i:
                            what()
                ins.then_inc(pe_job, 1)

            def paired(t, name, src, h):
                turns(f"{name}_{t}_{h}", [src[:, 2 * j:2 * j + 2, :] for j in range(h * 8, h * 8 + 8)])

            def h_paired(t):
                for h in range(2):
                    wait_reader(pe, f"acc_{STEPS - 1}_{t}_{h}")
                    paired(t, "th", wc(coef[:, t, 3, :]), h)

            def x_paired(t):
                pe.wait_ge(x_again[t], 16)
                for h in range(2):
                    paired(t, "tx", wc(coef[:, t, 1, :]), h)

            def group_mean2(t):
                pe.wait_ge(mv_ready, t + 1)
                small(f"mean2_{t}", BT, pairavg[:, :, :, :].rearrange("p a b c -> p (a b c)"), mv[:, t, :, 0])

            def group_var2(t):
                pe.wait_ge(q_ready, t + 1)
                small(f"var2_{t}", BT, pairavg[:, :, :, :].rearrange("p a b c -> p (a b c)"), gn2[:, t, 2, :])

            def dense(t, halves):
                pe.wait_ge(odd_ready, 4 * (t + 1))
                for h in halves:
                    dst = take(f"cf_{t}_{h}")
                    for bank in range(2):
                        j0 = 4 * (2 * h + bank)
                        to = dst[:, bank * BANK:(bank + 1) * BANK].rearrange("p (r h) -> p r h", h=H)
                        steps = [(b, dy, part) for b in range(2) for dy in range(3) for part in (hi, lo)]
                        for i, (b, dy, part) in enumerate(steps):
                            rows = part[:, :].rearrange("p (r h) -> p r h", h=HP)
                            ins = mm(to, dense_m[:, b, dy, :], rows[:, (j0 + b) * BT:(j0 + b + 4) * BT, dy:dy + H],
                                     start=(i == 0), stop=(i == len(steps) - 1))
                    ins.then_inc(pe_job, 1)

            def out_natural(t):
                for h in range(2):
                    pe.wait_ge(sum_ready, 2 * t + h + 1)
                    turns(f"tb_{t}_{h}", [half(coef[:, t, 3, :], h)[:, j * 128:j * 128 + 128] for j in range(8)])

            blockm = block[:, :, :].rearrange("p a b -> p (a b)")
            spreadm = spread4[:, :, :].rearrange("p a b -> p (a b)")
            pe.wait_ge(spread_ready, 1)
            pe.wait_ge(taps_in, 32)
            small("wtaps", 2 * 9 * CG, spreadm, taps4[:, :, :, :].rearrange("p a k g -> p (a k g)"))
            pe.wait_ge(near_ready, 1)
            pe.wait_ge(xsum_ready, 1)
            small("mean_0", GROUPS, blockm, gsum[:, 0, 0, :])
            pe.wait_ge(bn4_ready, 1)
            small("bnrow", 4 * CG, spreadm, bn4o[:, :, :].rearrange("p a g -> p (a g)"))
            pe.wait_ge(vsum_ready, 1)
            small("var_0", GROUPS, blockm, gsum[:, 0, 2, :])
            pe.wait_ge(xsum_ready, 2)
            small("mean_1", GROUPS, blockm, gsum[:, 1, 0, :])
            pe.wait_ge(ident_ready, 1)
            to_depthwise(0, 0)
            to_depthwise(0, 1)
            pe.wait_ge(sobel_m_ready, 4)
            for g in range(2):
                for h in range(2):
                    sobel(0, g, h)
            depthwise(0, 0, 0)
            pe.wait_ge(vsum_ready, 2)
            small("var_1", GROUPS, blockm, gsum[:, 1, 2, :])
            depthwise(0, 0, 1)
            depthwise(0, 1, 0)
            back(0, 0, 0)
            depthwise(0, 1, 1)
            back(0, 0, 1)
            back(0, 1, 0)
            back(0, 1, 1)
            pe.wait_ge(ones_ready, 1)
            pe.wait_ge(wabs_ready, 1)
            small("wsum", 1, ones[:, :], wred[:, 0:1])
            to_depthwise(1, 0)
            to_depthwise(1, 1)
            pe.wait_ge(kept_ready, 1)
            small("alpha", 2, ones[:, :], wred[:, 3:5])
            depthwise(1, 0, 0)
            depthwise(1, 0, 1)
            for g in range(2):
                for h in range(2):
                    sobel(1, g, h)
            depthwise(1, 1, 0)
            back(1, 0, 0)
            depthwise(1, 1, 1)
            back(1, 0, 1)
            back(1, 1, 0)
            back(1, 1, 1)
            for k, t in ORDER:
                if (k, t) == (STEPS - 2, 1):
                    sum_products(t, k, ((1, lambda: h_paired(0)), (3, lambda: x_paired(0))))
                    pe.wait_ge(pairavg_ready, 2)
                    group_mean2(0)
                    group_var2(0)
                else:
                    sum_products(t, k)
            pe.wait_ge(dense_m_ready, 6)
            dense(0, (0,))
            h_paired(1)
            x_paired(1)
            dense(0, (1,))
            group_mean2(1)
            group_var2(1)
            out_natural(0)
            dense(1, (0, 1))
            out_natural(1)
    return nc


_NAMES = ["x", "L0_conv_wg", "L0_conv_wg1", "L0_conv_g_gamma", "L0_conv_g1_gamma", "L0_conv_g_beta", "L0_conv_g1_beta",
          "L0_conv_g_mean", "L0_conv_g1_mean", "L0_conv_g_var", "L0_conv_g1_var", "L0_conv_out_gamma",
          "L0_conv_out_beta", "L0_conv_out_mean", "L0_conv_out_var", "L1_conv_b", "L1_conv_W"]


def kernel(**inputs):
    import numpy as _np
    import concourse.bacc as _bacc
    from concourse import mybir as _mybir
    from concourse.bass_utils import run_bass_kernel_spmd as _run

    nc = _bacc.Bacc("TRN2", target_bir_lowering=False, num_devices=1)
    arrays, ap = {}, {}
    for name in _NAMES:
        a = _np.ascontiguousarray(inputs[name])
        arrays[f"in_{name}"] = a
        ap[name] = nc.dram_tensor(f"in_{name}", a.shape, _mybir.dt.from_np(a.dtype), kind="ExternalInput").ap()
    out = nc.dram_tensor("out", (B, H, W, C), _mybir.dt.float32, kind="ExternalOutput").ap()
    bn_rows = [ap[n].rearrange("(a g) -> a g", g=CG) for n in _NAMES[3:11]]
    out_cols = [ap[n].rearrange("(c o) -> c o", o=1) for n in _NAMES[11:16]]
    network(nc, ap["x"], ap["L0_conv_wg"], ap["L0_conv_wg1"], bn_rows, out_cols, ap["L1_conv_W"], out)
    r = _run(nc, [arrays], core_ids=[0])
    return r.results[0]["out"]
```

```python
from contextlib import ExitStack

from concourse import mybir

B, H, W, C = 8, 32, 32, 64
TILES = 2
BT = B // TILES
N = W * C
HALF = N // 2
BANK = 512
CP = 4
CG = C // CP
PITCH = C + 2
ROWS = W + 2
STEPS = 5
DT = 0.2
BN_EPS, GN1_EPS, GN2_EPS = 1e-3, 1e-5, 1e-5
GROUPS = 32
PER_GROUP = H * W * (C // GROUPS)
PAIRS = W // 2
HP = H + 2
NCOEF = 7
A0, AE, FS, AXM, AXP, AYM, AYP = 1, 3, 0, 6, 4, 2, 5
RING = 3
SLOTS = 4
ORDER = [(0, 0), (1, 0), (0, 1), (2, 0), (1, 1), (3, 0), (2, 1), (4, 0), (3, 1), (4, 1)]
S = 1.0 / (2.0 * DT)
FAR = 200


def job_table():
    early = ["wtaps", "mean_0", "bnrow", "var_0", "mean_1", "t2_0_0", "t2_0_1",
             "gy_0_0", "gy_0_1", "gx_0_0", "gx_0_1", "cv_0_0_0", "var_1", "cv_0_0_1",
             "cv_0_1_0", "bk_0_0_0", "cv_0_1_1", "bk_0_0_1", "bk_0_1_0", "bk_0_1_1", "wsum", "t2_1_0", "t2_1_1",
             "cv_1_0_0", "cv_1_0_1", "alpha", "gy_1_0", "gy_1_1", "gx_1_0", "gx_1_1",
             "cv_1_1_0", "bk_1_0_0", "cv_1_1_1", "bk_1_0_1", "bk_1_1_0", "bk_1_1_1"]
    jobs = [(name, i % SLOTS) for i, name in enumerate(early)]

    assert {slot for _, slot in jobs[-2:]} == {2, 3}

    def halves(name, t):
        return [(f"{name}_{t}_{h}", 2 * t + h) for h in range(2)]

    jobs += halves("dv", 1)
    for k, t in ORDER:
        if (k, t) == (STEPS - 2, 1):
            jobs += halves("th", 0) + halves("tx", 0)
        if (k, t) == (STEPS - 1, 1):
            jobs += [("mean2_0", 0), ("var2_0", 1)]
        jobs += [(f"acc_{k}_{t}_{h}", 2 * t + h) for h in range(2)]
    jobs += [("tx_1_0", 0), ("tx_1_1", 1)] + halves("th", 1)
    jobs += [("cf_0_0", 2), ("mean2_1", 0), ("var2_1", 1), ("cf_0_1", 3), ("tb_0_0", 0)]
    quarter_slot = (2, 3, 0, 1)
    for name in ("cf_1_0", "cf_1_1", "tb_0_1", "cf_1_2", "tb_1_0", "cf_1_3", "tb_1_1", "tb_1_2", "tb_1_3"):
        jobs.append((name, 1 if name == "tb_0_1" else quarter_slot[int(name[-1])]))
    return jobs


def network(nc, x, wg, wg1, bn_rows, out_cols, conv_w, out):
    f32, f32r, i32 = mybir.dt.float32, mybir.dt.float32r, mybir.dt.int32
    ALU, ACT, AX = mybir.AluOpType, mybir.ActivationFunctionType, mybir.AxisListType

    jobs = job_table()
    job_no = {name: i for i, (name, _) in enumerate(jobs)}
    slot_of = dict(jobs)
    uses_before, seen = {}, [0] * SLOTS
    for name, slot in jobs:
        uses_before[name] = seen[slot]
        seen[slot] += 1

    with ExitStack() as ctx:
        def sb(name, shape, dt=f32):
            return ctx.enter_context(nc.sbuf_tensor(name, shape, dt))

        def sem(name):
            return ctx.enter_context(nc.semaphore(name))

        coef = sb("coef", [128, TILES, NCOEF, N])
        state = sb("state", [128, TILES, 2, ROWS, PITCH])
        ring = sb("ring", [128, RING, N])
        hi = sb("hi", [128, (PAIRS + 1) * BT * HP], f32r)
        lo = sb("lo", [128, (PAIRS + 1) * BT * HP], f32r)
        sobel_m = sb("sobel_m", [128, 4, 128], f32r)
        dense_m = sb("dense_m", [128, 2, 3, 128], f32r)
        ident = sb("ident", [128, 128])
        block = sb("block", [128, CP, 32])
        smooth = sb("smooth", [128, CP, 32])
        diff = sb("diff", [128, CP, 32])
        near = sb("near", [128, 3, CP, 32])
        tapmask = sb("tapmask", [128, 3, 32])
        spread4 = sb("spread4", [CP, CP, 32])
        pairavg = sb("pairavg", [128, 2, GROUPS, 2])
        ones = sb("ones", [128, 128])
        taps4 = sb("taps4", [CP, 2, 9, CG])
        taps = sb("taps", [128, 2 * 9 * CG])
        bn4 = sb("bn4", [CP, 4, 2 * CG])
        bn4w = sb("bn4w", [CP, 3, 2 * CG])
        bn4o = sb("bn4o", [CP, 2, 2 * CG])
        bnp = sb("bnp", [128, 2, 2, CG])
        outp = sb("outp", [128, 5])
        outw = sb("outw", [128, 4])
        gsum = sb("gsum", [128, TILES, 5, GROUPS])
        rs_in = sb("rs_in", [128, GROUPS])
        rs_ln = sb("rs_ln", [128, GROUPS])
        rs_y = sb("rs_y", [128, GROUPS])
        rs_t = sb("rs_t", [128, GROUPS])
        wred = sb("wred", [128, 8])
        stats = sb("stats", [128, BT, 2, 6])
        mv = sb("mv", [128, TILES, BT, 2])
        minus1 = sb("minus1", [128, 1])
        gn2 = sb("gn2", [128, TILES, 6, BT])
        psum = ctx.enter_context(nc.psum_tensor("psum", [128, SLOTS, HALF], f32))

        x_in = [ring[:, t, :] for t in range(TILES)]
        square = ring[:, 2, :]
        compact = coef[:, 0, 5:7, :].rearrange("p a n -> p (a n)")[:, 0:96 * 32].rearrange("p (m w) -> p m w", w=32)
        taps_m = coef[:, 1, 0:6, :].rearrange("p a n -> p (a n)").rearrange("p (m n) -> p m n", n=128)
        wl = coef[:, 1, 6, 0:9 * C]
        wabs = coef[:, 1, 6, 9 * C:18 * C]
        wtern = coef[:, 1, 6, 18 * C:27 * C]
        sT = [state[:, t, 1, :, :].rearrange("p r q -> p (r q)")[:, 0:N] for t in range(TILES)]
        gT = [ring[:, 0, :], ring[:, 1, :]]
        minus_ident = diff[:, :, :].rearrange("p a b -> p (a b)")
        six_ident = smooth[:, :, :].rearrange("p a b -> p (a b)")
        y_first = [coef[:, 0, 4, :], ring[:, 2, :]]
        gN = [coef[:, t, 6, :] for t in range(TILES)]
        g1N = sT

        def h_at(t, k, dw=0, dc=0, w0=0, w1=W):
            return state[:, t, k % 2, 1 + dw + w0:1 + dw + w1, 1 + dc:1 + dc + C]

        def wc(ap):
            return ap.rearrange("p (w c) -> p w c", c=C)

        def half(ap, h):
            return ap[:, h * HALF:(h + 1) * HALF]

        def expansion(conv, q):
            p, m = slice(32 * q, 32 * q + 32), slice(48 * conv, 48 * conv + 48)
            return taps_m[p, m, 32 * q:32 * q + 32], compact[p, m, :]

        out_parts = (2, 4)

        def part(ap, t, i):
            n = N // out_parts[t]
            return ap[:, i * n:(i + 1) * n]

        def odd_pairs(t):
            return coef[:, t, 3:5, :].rearrange("p a n -> p (a n)")[:, 0:(PAIRS + 1) * BT * H]

        def by_rows(ap, t, i):
            first, h = (PAIRS // out_parts[t] + 1) * BT, H if ap.shape[-1] == (PAIRS + 1) * BT * H else HP
            return ap.rearrange("p (r h) -> p r h", h=h)[:, slice(0, first) if i == 0 else slice(first, None)]

        def slot_ap(name):
            return psum[:, slot_of[name], :]

        taps_in, bn_in, outp_in, wl_in = sem("taps_in"), sem("bn_in"), sem("outp_in"), sem("wl_in")
        x_loaded, x_loaded0b = [sem("x_loaded0"), sem("x_loaded1")], sem("x_loaded0b")
        bn_var_in = sem("bn_var_in")
        x_again = [sem("x_again0"), sem("x_again1")]
        out_stored = sem("out_stored")
        pe_job = sem("pe_job")
        slot_free = [sem(f"slot_free{q}") for q in range(SLOTS)]
        pool_step, dve_step, act_step = sem("pool_step"), sem("dve_step"), sem("act_step")
        spread_ready, near_ready, ident_ready, sobel_src = (sem(n) for n in (
            "spread_ready", "near_ready", "ident_ready", "sobel_src"))
        ones_ready, pairavg_ready, zero_ready = sem("ones_ready"), sem("pairavg_ready"), sem("zero_ready")
        compact_ready, taps_m_ready, taps_m_too = sem("compact_ready"), sem("taps_m_ready"), sem("taps_m_too")
        xsum_ready, xm_ready, sq_ready, vsum_ready = (sem(n) for n in (
            "xsum_ready", "xm_ready", "sq_ready", "vsum_ready"))
        s_ready, s_hi, s_lo, s_halo = sem("s_ready"), sem("s_hi"), sem("s_lo"), sem("s_halo")
        s_reordered, den_const = sem("s_reordered"), sem("den_const")
        rs_asked, rs_given = sem("rs_asked"), sem("rs_given")
        bn4_ready, outw_ready = sem("bn4_ready"), sem("outw_ready")
        sobel_m_ready, dense_m_ready = sem("sobel_m_ready"), sem("dense_m_ready")
        u_ready, y_ready, sb_ready, d_ready = (sem(n) for n in ("u_ready", "y_ready", "sb_ready", "d_ready"))
        rest_ready, minus_ready = sem("rest_ready"), sem("minus_ready")
        shifted_ready = sem("shifted_ready")
        centre_ready, source_ready = sem("centre_ready"), sem("source_ready")
        product, ring_free = sem("product"), sem("ring_free")
        halo_ready, s_scaled = sem("halo_ready"), sem("s_scaled")
        wabs_ready, kept_ready, alpha_ready, tern_ready = (sem(n) for n in (
            "wabs_ready", "kept_ready", "alpha_ready", "tern_ready"))
        mv_ready, q_ready, norm_ready, xn_ready, xh_ready, xl_ready = (sem(n) for n in (
            "mv_ready", "q_ready", "norm_ready", "xn_ready", "xh_ready", "xl_ready"))
        pads_ready, sum_ready = sem("pads_ready"), sem("sum_ready")
        edges_ready, xn_too = sem("edges_ready"), sem("xn_too")

        def wait_job(eng, name):
            eng.wait_ge(pe_job, job_no[name] + 1)

        def wait_reader(eng, name):
            eng.wait_ge(slot_free[slot_of[name]], uses_before[name] + 1)

        def frees(ins, name):
            ins.then_inc(slot_free[slot_of[name]], 1)

        def direct(k, t):
            return (k, t) == (STEPS - 2, 1)

        def products_of(k, t):
            return 4 if k == 0 or direct(k, t) else 5

        def products_through(k, t):
            return sum(products_of(kk, tt) for kk, tt in ORDER[:ORDER.index((k, t)) + 1])

        def states_through(k, t):
            return sum(kk < STEPS - 1 for kk, _ in ORDER[:ORDER.index((k, t)) + 1])

        x_nat = x.rearrange("(t b) h w c -> t (b h) (w c)", t=TILES)
        out_nat = out.rearrange("(t b) h w c -> t (b h) (w c)", t=TILES)

        blk = ctx.enter_context(nc.Block())

        @blk.sync
        def _(sp):
            for h in range(2):
                sp.dma_start(half(x_in[0], h), half(x_nat[0], h)).then_inc((x_loaded[0], x_loaded0b)[h], 16)
            for conv, src in enumerate((wg, wg1)):
                sp.dma_start(taps4[:, conv, :, :],
                             src.rearrange("y x (a g) -> a (y x) g", g=CG)).then_inc(taps_in, 16)
            sp.dma_start(x_in[1], x_nat[1]).then_inc(x_loaded[1], 16)
            sp.wait_ge(x_loaded[1], 16)
            for k in range(2):
                sp.dma_start(wl[64 * k:64 * k + 64, :].rearrange("i (k o) -> i k o", o=C),
                             conv_w.rearrange("y x i o -> i (y x) o")).then_inc(wl_in, 16)
            for i, col in enumerate(out_cols):
                for k in range(2):
                    sp.dma_start(outp[64 * k:64 * k + 64, i:i + 1], col).then_inc(outp_in, 16)
            for t in range(TILES):
                sp.wait_ge(rest_ready, t + 1)
                sp.dma_start(coef[:, t, 1, :], x_nat[t]).then_inc(x_again[t], 16)
            for t in range(TILES):
                for h in range(out_parts[t]):
                    wait_reader(sp, f"tb_{t}_{h}")
                    sp.dma_start(part(out_nat[t], t, h), part(coef[:, t, 4, :], t, h)).then_inc(out_stored, 16)
            sp.wait_ge(out_stored, 16 * sum(out_parts))

        @blk.gpsimd
        def _(pool):
            steps = [0]

            def then(ins):
                steps[0] += 1
                ins.then_inc(pool_step, 1)
                pool.wait_ge(pool_step, steps[0])

            def select(ap, pattern, base, mult, fill, op=ALU.not_equal):
                return nc.gpsimd.affine_select(out=ap, in_=ap, pattern=pattern, compare_op=op, fill=fill, base=base,
                                               channel_multiplier=mult)

            def times_block(ap):
                return nc.gpsimd.tensor_tensor(ap, ap, block[:, :, :], ALU.mult)

            nc.gpsimd.memset(minus1[:, :], -1.0).then_inc(den_const, 1)
            then(nc.gpsimd.memset(spread4[:, :, :], 0.0))
            select(spread4[:, :, :], [[-1, CP], [0, 32]], 0, 1, 1.0).then_inc(spread_ready, 1)
            then(nc.gpsimd.memset(block[:, :, :], 1.0))
            then(select(block[:, :, :], [[-32, CP], [0, 32]], 0, 1, 0.0, ALU.is_ge))
            then(select(block[:, :, :], [[32, CP], [0, 32]], 31, -1, 0.0, ALU.is_ge))
            then(nc.gpsimd.memset(near[:, :, :, :], 0.0))
            for d in range(3):
                then(select(near[:, d, :, :], [[-32, CP], [-1, 32]], 1 - d, 1, 1.0))
                times_block(near[:, d, :, :]).then_inc(near_ready, 1)
            then(nc.gpsimd.memset(ident[:, :], 0.0))
            select(ident[:, :], [[-1, 128]], 0, 1, 1.0).then_inc(ident_ready, 1)
            then(nc.gpsimd.memset(smooth[:, :, :], 0.0))
            then(select(smooth[:, :, :], [[-32, CP], [-1, 32]], 0, 1, 2.0))
            then(select(smooth[:, :, :], [[-32, CP], [-1, 32]], -1, 1, 1.0))
            then(select(smooth[:, :, :], [[-32, CP], [-1, 32]], 1, 1, 1.0))
            then(times_block(smooth[:, :, :]))
            then(select(smooth[:, :, :], [[-32, CP], [FAR, 32]], -1, 1, 2.0))
            select(smooth[:, :, :], [[-32, CP], [FAR, 32]], -30 - 31 * FAR, 1, 2.0).then_inc(sobel_src, 1)
            then(nc.gpsimd.memset(diff[:, :, :], 0.0))
            then(select(diff[:, :, :], [[-32, CP], [-1, 32]], -1, 1, 1.0))
            then(select(diff[:, :, :], [[-32, CP], [-1, 32]], 1, 1, -1.0))
            then(times_block(diff[:, :, :]))
            then(select(diff[:, :, :], [[0, CP], [1, 32]], 0, 0, 0.0, ALU.is_gt))
            select(diff[:, :, :], [[0, CP], [-1, 32]], 31, 0, 0.0, ALU.is_gt).then_inc(sobel_src, 1)
            nc.gpsimd.memset(ones[:, :], 1.0).then_inc(ones_ready, 1)
            for conv in range(2):
                nc.gpsimd.memset(coef[:, 1, 3 * conv:3 * conv + 3, :].rearrange("p a n -> p (a n)"), 0.0)\
                    .then_inc(zero_ready, 1)
            nc.gpsimd.memset(dense_m[:, :, :, :].bitcast(f32), 0.0).then_inc(zero_ready, 1)
            then(nc.gpsimd.memset(pairavg[:, :, :, :], 0.25))
            for k in range(2):
                part = pairavg[64 * k:64 * k + 64, :, :, :]
                then(select(part, [[0, 2], [-2, GROUPS], [0, 2]], 0, 1, 0.0, ALU.is_ge))
                select(part, [[0, 2], [2, GROUPS], [0, 2]], 1, -1, 0.0, ALU.is_ge).then_inc(pairavg_ready, 1)
                pool.wait_ge(pairavg_ready, k + 1)
            wait_job(pool, "gx_1_1")
            nc.gpsimd.memset(hi[:, :].bitcast(f32), 0.0).then_inc(pads_ready, 1)
            nc.gpsimd.memset(lo[:, :].bitcast(f32), 0.0).then_inc(pads_ready, 1)
            for t in range(TILES):
                wait_job(pool, f"th_{t}_1")
                for k, column in enumerate((0, PAIRS)):
                    pool.wait_ge(pads_ready, 2)
                    if 2 * t + k:
                        pool.wait_ge(edges_ready, 2 * t + k)
                    nc.gpsimd.memset(odd_pairs(t)[64 * k:64 * k + 64, column * BT * H:(column + 1) * BT * H], 0.0)\
                        .then_inc(edges_ready, 1)

        @blk.scalar
        def _(act):
            steps, asked = [0], [0]

            def then(ins):
                steps[0] += 1
                ins.then_inc(act_step, 1)
                act.wait_ge(act_step, steps[0])

            def copy(dst, src, func=ACT.Copy, **kw):
                return nc.scalar.activation(dst, src, func, **kw)

            def rsqrt_first(p, n):
                asked[0] += 1
                act.wait_ge(rs_asked, asked[0])
                then(copy(rs_ln[0:p, 0:n], rs_in[0:p, 0:n], ACT.Ln))
                copy(rs_y[0:p, 0:n], rs_ln[0:p, 0:n], ACT.Exp, scale=-0.5).then_inc(rs_given, 1)

            def square_of(t):
                act.wait_ge(xm_ready, t + 1)
                copy(wc(square), h_at(t, 0), ACT.Square).then_inc(sq_ready, 1)

            def wrap(t, k, done):
                s = state[:, t, k % 2, :, :]
                copy(s[:, 0, 1:1 + C], s[:, W, 1:1 + C]).then_inc(done, 1)
                copy(s[:, W + 1, 1:1 + C], s[:, 1, 1:1 + C]).then_inc(done, 1)
                copy(s[:, 1:1 + W, 0:1], s[:, 1:1 + W, C:C + 1]).then_inc(done, 1)
                copy(s[:, 1:1 + W, C + 1:C + 2], s[:, 1:1 + W, 1:2]).then_inc(done, 1)

            def split_hi(t):
                act.wait_ge(s_ready, t + 1)
                wait_job(act, "gx_0_1")
                copy(wc(hi[:, 0:N]), h_at(t, 0)).then_inc(s_hi, 1)

            def reorder(t):
                act.wait_ge(s_ready, t + 1)
                copy(sT[t].rearrange("p (g a w) -> p g a w", a=CP, w=W),
                     h_at(t, 0).rearrange("p w (a g) -> p g a w", g=CG)).then_inc(s_reordered, 1)

            def to_depthwise(t, h):
                wait_job(act, f"t2_{t}_1")
                frees(copy(half(sT[t], h), slot_ap(f"t2_{t}_{h}")), f"t2_{t}_{h}")

            def sobel_square(t, g, h):
                name = f"{('gy', 'gx')[g]}_{t}_{h}"
                wait_job(act, name)
                frees(copy(half(coef[:, t, g, :], h), slot_ap(name), ACT.Square, scale=0.5 * S ** 0.5), name)

            def bn_bias(t, conv, h):
                name = f"cv_{t}_{conv}_{h}"
                wait_job(act, name)
                if t:
                    wait_job(act, f"bk_0_{conv}_1")
                for j in range(CG // 2):
                    cg = h * (CG // 2) + j
                    ins = copy(gT[conv][:, cg * 128:cg * 128 + 128], slot_ap(name)[:, j * 128:j * 128 + 128],
                               ACT.Identity, bias=bnp[:, 1, conv, cg:cg + 1])
                frees(ins, name)

            def to_natural(t, conv, h):
                name = f"bk_{t}_{conv}_{h}"
                wait_job(act, name)
                dst = (gN, g1N)[conv][t].rearrange("p (w a g) -> p w a g", a=CP, g=CG)
                src = slot_ap(name).rearrange("p (g a w) -> p w a g", a=CP, w=W)
                frees(copy(dst[:, :, :, h * (CG // 2):(h + 1) * (CG // 2)], src, ACT.Relu), name)

            def reciprocal_first(t):
                act.wait_ge(u_ready, t + 1)
                act.wait_ge(den_const, 1)
                then(copy(y_first[t], coef[:, t, 2, :], ACT.Ln, bias=minus1[:, 0:1]))
                copy(y_first[t], y_first[t], ACT.Exp, scale=-1.0).then_inc(y_ready, 1)

            def d_of(t):
                act.wait_ge(sb_ready, t + 1)
                copy(coef[:, t, 0, :], coef[:, t, 2, :], bias=1.0).then_inc(d_ready, 1)
                copy(coef[:, t, A0, :], coef[:, t, 2, :], scale=2.0, bias=1.0).then_inc(d_ready, 1)

            for i in (6, 7, 0, 1, 2, 3, 4, 5):
                act.dma_start(bn4[:, i // 2, (i % 2) * CG:(i % 2 + 1) * CG], bn_rows[i])\
                    .then_inc(bn_var_in if i >= 6 else bn_in, 16)
            nc.scalar.preload_act_table_set("natural_log_exp_and_others")
            wait_job(act, "wtaps")
            frees(copy(taps[:, :], slot_ap("wtaps")[:, 0:2 * 9 * CG]), "wtaps")
            rsqrt_first(CP, 2 * CG)
            square_of(0)
            wait_job(act, "bnrow")
            frees(copy(bnp[:, :, :, :].rearrange("p a b c -> p (a b c)"), slot_ap("bnrow")[:, 0:4 * CG]), "bnrow")
            act.wait_ge(sobel_src, 2)
            for i, (m, scale) in enumerate(((smooth, 1.0), (smooth, -1.0), (diff, 1.0), (diff, 2.0))):
                copy(sobel_m[:, i, :], m[:, :, :].rearrange("p a b -> p (a b)"), scale=scale)\
                    .then_inc(sobel_m_ready, 1)
            act.wait_ge(ident_ready, 1)
            act.wait_ge(sobel_m_ready, 4)
            copy(six_ident, ident[:, :], scale=(2.0 + 2 * DT) / (2 * DT)).then_inc(minus_ready, 1)
            copy(minus_ident, ident[:, :], scale=-1.0).then_inc(minus_ready, 1)
            rsqrt_first(128, GROUPS)
            reorder(0)
            to_depthwise(0, 0)
            to_depthwise(0, 1)

            def expand(conv):
                act.wait_ge(compact_ready, 1)
                act.wait_ge(zero_ready, conv + 1)
                for q in range(2):
                    copy(*expansion(conv, q)).then_inc(taps_m_ready, 1)

            sobel_square(0, 0, 0)
            sobel_square(0, 0, 1)
            expand(0)
            sobel_square(0, 1, 0)
            sobel_square(0, 1, 1)
            square_of(1)
            expand(1)
            rsqrt_first(128, GROUPS)
            reciprocal_first(0)
            bn_bias(0, 0, 1)
            split_hi(1)
            bn_bias(0, 1, 0)
            reorder(1)
            act.wait_ge(wl_in, 32)
            copy(wabs, wl, ACT.Abs, accum_out=wred[:, 0:1]).then_inc(wabs_ready, 1)
            wrap(0, 0, s_halo)
            to_natural(0, 0, 0)
            bn_bias(0, 1, 1)
            to_natural(0, 0, 1)
            to_natural(0, 1, 0)
            to_natural(0, 1, 1)
            to_depthwise(1, 0)
            to_depthwise(1, 1)
            d_of(0)
            wrap(1, 0, s_halo)
            bn_bias(1, 0, 0)
            bn_bias(1, 0, 1)
            for g in range(2):
                for h in range(2):
                    sobel_square(1, g, h)
            wait_reader(act, "gx_1_0")
            wait_reader(act, "gx_1_1")
            copy(coef[:, 1, 2, :], coef[:, 1, 1, :], bias=(1.0 + 2 * DT) * S).then_inc(shifted_ready, 1)
            act.wait_ge(tern_ready, 1)
            act.wait_ge(zero_ready, 3)
            tern = wtern.rearrange("p (y x o) -> p y x o", y=3, x=3)
            for b, k, m, dx in ((0, 0, 0, 0), (0, 1, 0, 1), (0, 1, 1, 0), (1, 0, 0, 2), (1, 0, 1, 1), (1, 1, 1, 2)):
                copy(dense_m[64 * k:64 * k + 64, b, :, 64 * m:64 * m + 64], tern[64 * k:64 * k + 64, :, dx, :])\
                    .then_inc(dense_m_ready, 1)
            bn_bias(1, 1, 0)
            reciprocal_first(1)
            act.wait_ge(dense_m_ready, 6)
            to_natural(1, 0, 0)
            to_natural(1, 0, 1)
            rsqrt_first(128, 1)
            to_natural(1, 1, 0)
            to_natural(1, 1, 1)
            d_of(1)

            def relu_bn_out(t, h):
                wait_job(act, f"th_{t}_{h}")
                frees(copy(half(coef[:, t, 0, :], h), slot_ap(f"th_{t}_{h}"), ACT.Relu, scale=outw[:, 2:3],
                           bias=outw[:, 3:4]), f"th_{t}_{h}")

            def normalise(t):
                act.wait_ge(norm_ready, t + 1)
                wait_job(act, f"th_{t}_1")
                x1 = coef[:, t, 2, :].rearrange("p (j b h) -> p j b h", b=BT, h=H)
                to = odd_pairs(t).rearrange("p (j b h) -> p j b h", b=BT, h=H)
                for b in range(BT - 1):
                    copy(to[0:64, 1:, b, :], x1[64:128, :, b, :], ACT.Identity, scale=gn2[64:128, t, 3, b:b + 1],
                         bias=gn2[64:128, t, 4, b:b + 1]).then_inc(xn_ready, 1)

            def upper_half(t):
                act.wait_ge(pads_ready, 2)
                act.wait_ge(edges_ready, 2 * (t + 1))
                act.wait_ge(xn_ready, (BT - 1) * (t + 1))
                act.wait_ge(xn_too, (BT + 1) * (t + 1))
                for h in range(2):
                    if t:
                        wait_job(act, f"cf_0_{h}")
                    copy(by_rows(hi[:, :], t, h)[:, :, 1:1 + H], by_rows(odd_pairs(t), t, h)).then_inc(xh_ready, 1)

            def relu_dense(t, h):
                act.wait_ge(alpha_ready, 1)
                name = f"cf_{t}_{h}"
                wait_job(act, name)
                frees(copy(part(coef[:, t, 0, :], t, h), part(slot_ap(name), t, 0), ACT.Relu, scale=wred[:, 7:8],
                           bias=outp[:, 4:5]), name)

            def take_out(t, h):
                name = f"tb_{t}_{h}"
                wait_job(act, name)
                frees(copy(part(coef[:, t, 4, :], t, h), part(slot_ap(name), t, 0)), name)

            for k, t in ORDER[:-1]:
                if k == 0:
                    act.wait_ge(product, products_through(0, t))
                    copy(h_at(t, 0), h_at(t, 0), scale=1.0 + DT).then_inc(s_scaled, 1)
                if k < STEPS - 1:
                    if k == STEPS - 2 and t == 1:
                        act.wait_ge(outw_ready, 1)
                        relu_bn_out(0, 0)
                        relu_bn_out(0, 1)
                    if k == 0:
                        for h in range(2):
                            name = f"acc_0_{t}_{h}"
                            wait_job(act, name)
                            frees(copy(h_at(t, 1, w0=h * W // 2, w1=(h + 1) * W // 2), wc(slot_ap(name))), name)
                    wait_reader(act, f"acc_{k}_{t}_0")
                    wait_reader(act, f"acc_{k}_{t}_1")
                    wrap(t, k + 1, halo_ready)
            rsqrt_first(128, BT)
            normalise(0)
            upper_half(0)
            relu_bn_out(1, 0)
            relu_bn_out(1, 1)
            relu_dense(0, 0)
            rsqrt_first(128, BT)
            normalise(1)
            upper_half(1)
            relu_dense(0, 1)
            take_out(0, 0)
            relu_dense(1, 0)
            relu_dense(1, 1)
            take_out(0, 1)
            relu_dense(1, 2)
            take_out(1, 0)
            relu_dense(1, 3)
            for q in range(1, 4):
                take_out(1, q)

        @blk.vector
        def _(dve):
            steps, asked = [0], [0]
            V = nc.vector

            def then(ins):
                steps[0] += 1
                ins.then_inc(dve_step, 1)
                dve.wait_ge(dve_step, steps[0])

            def mark(ins):
                steps[0] += 1
                ins.then_inc(dve_step, 1)
                value = steps[0]
                return lambda: dve.wait_ge(dve_step, value)

            def signal(ins, done, value):
                ins.then_inc(done, 1)
                dve.wait_ge(done, value)

            def stt(out_ap, in0, scalar, in1, op0, op1):
                return V.scalar_tensor_tensor(out=out_ap, in0=in0, scalar=scalar, in1=in1, op0=op0, op1=op1)

            def leave(name):
                frees(V.memset(wred[:, 6:7], 0.0), name)

            def ask_rsqrt(ask):
                asked[0] += 1
                signal(ask, rs_asked, asked[0])

            def rsqrt(p, n, dst, ask=None):
                if ask is not None:
                    ask_rsqrt(ask)
                dve.wait_ge(rs_given, asked[0])
                y, v, a = rs_y[0:p, 0:n], rs_in[0:p, 0:n], rs_t[0:p, 0:n]
                then(V.tensor_tensor(a, y, y, ALU.mult))
                then(V.tensor_tensor(a, a, v, ALU.mult))
                then(V.tensor_scalar(a, a, -0.5, 1.5, ALU.mult, ALU.add))
                then(V.tensor_tensor(dst, y, a, ALU.mult))

            def over_w(ap32):
                return ap32.unsqueeze(1).unsqueeze(3).broadcast_to([128, W, GROUPS, 2])

            def grouped(ap):
                return ap.rearrange("p w (g c) -> p w g c", c=2)

            def sum_x(t):
                for h in range(2 - t):
                    dve.wait_ge((x_loaded[t], x_loaded0b)[h], 16)
                    src = half(x_in[0], h) if t == 0 else x_in[1]
                    V.tensor_reduce(gsum[:, t, (0, 4)[h], :], src.rearrange("p (w g c) -> p g w c", g=GROUPS, c=2),
                                    AX.XY, ALU.add).then_inc(xsum_ready, 1)

            def mean_of(t):
                wait_job(dve, f"mean_{t}")
                frees(V.tensor_scalar(gsum[:, t, 1, :], slot_ap(f"mean_{t}")[:, 0:GROUPS], 1.0 / PER_GROUP, None,
                                      ALU.mult), f"mean_{t}")

            def centre(t):
                wait_reader(dve, f"mean_{t}")
                signal(V.tensor_tensor(grouped(h_at(t, 0)), grouped(wc(x_in[t])), over_w(gsum[:, t, 1, :]),
                                       ALU.subtract), xm_ready, t + 1)

            def sum_squares(t):
                dve.wait_ge(sq_ready, t + 1)
                signal(V.tensor_reduce(gsum[:, t, 2, :], square.rearrange("p (w g c) -> p g w c", g=GROUPS, c=2),
                                       AX.XY, ALU.add), vsum_ready, t + 1)

            def scale_s(t):
                wait_job(dve, f"var_{t}")
                ask = V.tensor_scalar(rs_in[:, :], slot_ap(f"var_{t}")[:, 0:GROUPS], 1.0 / PER_GROUP, GN1_EPS,
                                      ALU.mult, ALU.add)
                rsqrt(128, GROUPS, gsum[:, t, 3, :], ask)
                s = grouped(h_at(t, 0))
                leave(f"var_{t}")
                signal(V.tensor_tensor(s, s, over_w(gsum[:, t, 3, :]), ALU.mult), s_ready, t + 1)

            def split_lo(t):
                dve.wait_ge(s_hi, t + 1)
                signal(V.tensor_tensor(wc(lo[:, 0:N]), h_at(t, 0), wc(hi[:, 0:N].bitcast(f32)), ALU.subtract),
                       s_lo, t + 1)

            sum_x(0)
            dve.wait_ge(near_ready, 3)
            then(V.tensor_reduce(tapmask[:, :, :], near[:, :, :, :].rearrange("p d a w -> p d w a"), AX.X, ALU.add))

            dve.wait_ge(bn_var_in, 16 * 2)
            gamma, beta, mean = bn4[:, 0, :], bn4[:, 1, :], bn4[:, 2, :]
            ask_rsqrt(V.tensor_scalar(rs_in[0:CP, 0:2 * CG], bn4[:, 3, :], BN_EPS, None, ALU.add))
            mean_of(0)
            centre(0)
            rsqrt(CP, 2 * CG, bn4w[:, 0, :])
            dve.wait_ge(bn_in, 16 * 6)
            then(V.tensor_tensor(bn4w[:, 1, :], bn4w[:, 0, :], gamma, ALU.mult))
            then(V.tensor_tensor(bn4w[:, 2, :], bn4w[:, 1, :], mean, ALU.mult))
            then(V.tensor_tensor(bn4w[:, 2, :], beta, bn4w[:, 2, :], ALU.subtract))
            signal(V.tensor_scalar(bn4o[:, :, :], bn4w[:, 1:3, :], DT, None, ALU.mult), bn4_ready, 1)

            sum_squares(0)
            sum_x(1)
            scale_s(0)
            mean_of(1)
            signal(V.tensor_copy(wc(hi[:, 0:N]), h_at(0, 0)), s_hi, 1)
            split_lo(0)

            wait_reader(dve, "wtaps")
            wait_reader(dve, "bnrow")
            tv2 = taps[:, :].rearrange("p (v k g) -> p v k g", v=2, g=CG)
            then(V.tensor_tensor(tv2, tv2, bnp[:, 0, :, :].unsqueeze(2).broadcast_to([128, 2, 9, CG]), ALU.mult))
            m4 = compact.rearrange("p (k g) w -> p k g w", g=CG)
            tv = taps[:, :].rearrange("p (k x g) -> p k x g", x=3, g=CG)

            def tap(d):
                return tv[:, :, d, :].unsqueeze(3).broadcast_to([128, 6, CG, 32])

            def mask(d):
                return tapmask[:, d, :].unsqueeze(1).unsqueeze(1).broadcast_to([128, 6, CG, 32])

            then(V.tensor_tensor(m4, tap(1), mask(1), ALU.mult))
            then(V.copy_predicated(m4, mask(0).bitcast(i32), tap(0)))
            signal(V.copy_predicated(m4, mask(2).bitcast(i32), tap(2)), compact_ready, 1)

            def expand(conv):
                dve.wait_ge(zero_ready, conv + 1)
                for q in range(2, CP):
                    V.tensor_copy(*expansion(conv, q)).then_inc(taps_m_too, 1)

            expand(0)
            centre(1)
            expand(1)
            sum_squares(1)

            def ternary():
                wait_job(dve, "wsum")
                ins = V.tensor_scalar(wred[:, 1:2], slot_ap("wsum")[:, 0:1], 1.0 / (2 * 9 * C * C), 0.7, ALU.mult,
                                      ALU.mult)
                frees(ins, "wsum")
                wait_reader(dve, "wsum")
                then(V.tensor_scalar(wred[:, 2:3], wred[:, 1:2], -1.0, None, ALU.mult))
                then(V.tensor_scalar(wtern, wabs, wred[:, 1:2], None, ALU.is_gt))
                then(V.tensor_reduce(wred[:, 4:5], wtern, AX.X, ALU.add))
                signal(V.scalar_tensor_tensor(out=wtern, in0=wabs, scalar=wred[:, 1:2], in1=wabs, op0=ALU.is_gt,
                                              op1=ALU.mult, accum_out=wred[:, 3:4]), kept_ready, 1)
                then(V.tensor_scalar(wabs, wl, wred[:, 2:3], None, ALU.is_le))
                signal(stt(wtern, wl, wred[:, 1:2], wabs, ALU.is_ge, ALU.subtract), tern_ready, 1)


            def denominator(t):
                for h in range(2):
                    wait_reader(dve, f"gy_{t}_{h}")
                    wait_reader(dve, f"gx_{t}_{h}")
                if t == 0:
                    then(V.tensor_scalar(coef[:, t, 2, :], coef[:, t, 1, :], (1.0 + 2 * DT) * S, None, ALU.add))
                else:
                    dve.wait_ge(shifted_ready, 1)
                signal(stt(coef[:, t, 2, :], coef[:, t, 0, :], (1.0 + 2 * DT) * S, coef[:, t, 2, :], ALU.add,
                           ALU.mult), u_ready, t + 1)

            def newton(t):
                c = [coef[:, t, i, :] for i in range(NCOEF)]
                dve.wait_ge(y_ready, t + 1)
                if t:
                    wait_job(dve, "cv_1_1_1")
                then(stt(c[3], c[2], -1.0, y_first[t], ALU.add, ALU.mult))
                then(stt(c[3], c[3], -2.0, y_first[t], ALU.add, ALU.mult))

            def diffusivities(t):
                c = [coef[:, t, i, :] for i in range(NCOEF)]
                then(stt(c[4], c[1], S, c[3], ALU.add, ALU.mult))
                if t == 0:
                    dve.wait_ge(taps_m_ready, 4)
                then(stt(c[5], c[0], S, c[3], ALU.add, ALU.mult))
                signal(V.tensor_tensor(c[2], c[4], c[5], ALU.add), sb_ready, t + 1)

            def divergence(t):
                for h in range(2):
                    wait_reader(dve, f"bk_{t}_0_{h}")
                    wait_reader(dve, f"bk_{t}_1_{h}")
                g, g1, e, e1 = wc(gN[t]), wc(g1N[t]), wc(coef[:, t, 3, :]), wc(coef[:, t, 2, :])
                V.tensor_tensor(e[:, 1:W - 1, :], g[:, 0:W - 2, :], g[:, 2:W, :], ALU.subtract)
                V.tensor_tensor(e[:, 0, :], g[:, W - 1, :], g[:, 1, :], ALU.subtract)
                then(V.tensor_tensor(e[:, W - 1, :], g[:, W - 2, :], g[:, 0, :], ALU.subtract))
                dve.wait_ge(d_ready, 2 * t + 2)
                V.tensor_tensor(e1[:, :, 1:C - 1], g1[:, :, 0:C - 2], g1[:, :, 2:C], ALU.subtract)
                V.tensor_tensor(e1[:, :, 0:1], g1[:, :, C - 1:C], g1[:, :, 1:2], ALU.subtract)
                then(V.tensor_tensor(e1[:, :, C - 1:C], g1[:, :, C - 2:C - 1], g1[:, :, 0:1], ALU.subtract))
                then(V.tensor_tensor(coef[:, t, 3, :], coef[:, t, 3, :], coef[:, t, 2, :], ALU.add))
                then(stt(coef[:, t, AE, :], coef[:, t, 3, :], -1.0, coef[:, t, 0, :], ALU.mult, ALU.mult))

            def divergence_taken(t):
                dve.wait_ge(d_ready, 2 * t + 2)
                for h in range(2):
                    name = f"dv_{t}_{h}"
                    wait_job(dve, name)
                    frees(stt(half(coef[:, t, AE, :], h), slot_ap(name), -1.0, half(coef[:, t, 0, :], h), ALU.mult,
                              ALU.mult), name)
                for h in range(2):
                    wait_reader(dve, f"dv_{t}_{h}")

            def over_channels(t):
                dve.wait_ge(d_ready, 2 * t + 2)
                then(V.tensor_tensor(coef[:, t, AYM, :], g1N[t], coef[:, t, 0, :], ALU.mult))
                then(V.tensor_tensor(coef[:, t, AYP, :], coef[:, t, AYM, :], coef[:, t, 5, :], ALU.subtract))
                return mark(stt(coef[:, t, AYM, :], coef[:, t, AYM, :], -2.0, coef[:, t, AYP, :], ALU.mult, ALU.add))

            def scaled_g(t):
                return mark(V.tensor_tensor(coef[:, t, 6, :], coef[:, t, 6, :], coef[:, t, 0, :], ALU.mult))

            def first_centre(t):
                stt(h_at(t, 1), wc(coef[:, t, AE, :]), -1.0, h_at(t, 0), ALU.add, ALU.mult).then_inc(centre_ready, 1)

            def source(t):
                stt(wc(coef[:, t, FS, :]), wc(coef[:, t, 0, :]), 2 * DT, h_at(t, 0), ALU.mult, ALU.mult)\
                    .then_inc(source_ready, 1)

            def plus_columns(t):
                return mark(V.tensor_tensor(coef[:, t, AXP, :], coef[:, t, 6, :], coef[:, t, 4, :], ALU.subtract))

            def minus_columns(t):
                return mark(stt(coef[:, t, AXM, :], coef[:, t, 6, :], -2.0, coef[:, t, AXP, :], ALU.mult, ALU.add))

            made = [0]
            sum_ends = {products_through(k, t): (k, t) for k in range(STEPS) for t in range(TILES)}

            def wait_summed(n):
                if n in sum_ends:
                    k, t = sum_ends[n]
                    wait_job(dve, f"acc_{k}_{t}_1")
                else:
                    dve.wait_ge(ring_free, n - sum(end < n for end in sum_ends))

            def multiply(t, k, a, dw, dc):
                slot = made[0] % RING
                if (k, t) == ORDER[0]:
                    wait_job(dve, "bk_1_1_1")
                if made[0] >= RING:
                    wait_summed(made[0] - RING + 1)
                made[0] += 1
                V.tensor_tensor(wc(ring[:, slot, :]), wc(coef[:, t, a, :]), h_at(t, k, dw, dc), ALU.mult)\
                    .then_inc(product, 1)

            rest_made = {}

            def rest(t, k):
                old = h_at(t, k + 1)
                ins = None
                if k:
                    dve.wait_ge(product, products_through(k - 1, t))
                if k == 1:
                    dve.wait_ge(s_scaled, t + 1)
                    ins = stt(old, wc(coef[:, t, A0, :]), DT / (1.0 + DT), old, ALU.add, ALU.mult)
                elif k > 1:
                    ins = V.tensor_tensor(old, old, wc(coef[:, t, A0, :]), ALU.mult)
                    if k == STEPS - 1:
                        signal(ins, rest_ready, t + 1)
                    else:
                        then(ins)
                    dve.wait_ge(source_ready, t + 1)
                    ins = V.tensor_tensor(old, old, wc(coef[:, t, FS, :]), ALU.add)
                rest_made[t] = mark(ins) if ins else lambda: None

            def total(t, k):
                rest_made[t]()
                for h in range(2):
                    name = f"acc_{k}_{t}_{h}"
                    wait_job(dve, name)
                    old = h_at(t, k + 1, w0=h * W // 2, w1=(h + 1) * W // 2)
                    new = old if k < STEPS - 1 else wc(half(coef[:, t, 3, :], h))
                    frees(V.tensor_tensor(new, wc(slot_ap(name)), old, ALU.add), name)

            def residual(t, before_stats=lambda: None):
                for h in range(2):
                    wait_reader(dve, f"th_{t}_{h}")
                    wait_job(dve, f"tx_{t}_{h}")
                    frees(V.tensor_tensor(half(coef[:, t, 2, :], h), slot_ap(f"tx_{t}_{h}"),
                                          half(coef[:, t, 0, :], h), ALU.add), f"tx_{t}_{h}")
                    wait_reader(dve, f"tx_{t}_{h}")
                    if h == 1:
                        before_stats()
                    x1 = half(coef[:, t, 2, :], h).rearrange("p (j b h) -> p j b h", b=BT, h=H)
                    for b in range(BT):
                        ins = V.bn_stats(stats[:, b, h, :], x1[:, :, b, :])
                then(ins)
                for b in range(BT):
                    ins = V.bn_aggr(mv[:, t, b, :], stats[:, b, :, :].rearrange("p a s -> p (a s)"))
                signal(ins, mv_ready, t + 1)

            def spread(t):
                wait_job(dve, f"mean2_{t}")
                frees(V.tensor_copy(gn2[:, t, 0, :], slot_ap(f"mean2_{t}")[:, 0:BT]), f"mean2_{t}")
                wait_reader(dve, f"mean2_{t}")
                then(V.tensor_tensor(gn2[:, t, 1, :], mv[:, t, :, 0], gn2[:, t, 0, :], ALU.subtract))
                then(V.tensor_tensor(gn2[:, t, 1, :], gn2[:, t, 1, :], gn2[:, t, 1, :], ALU.mult))
                signal(V.tensor_tensor(gn2[:, t, 2, :], mv[:, t, :, 1], gn2[:, t, 1, :], ALU.add), q_ready, t + 1)

            def second_norm(t):
                wait_job(dve, f"var2_{t}")
                rsqrt(128, BT, gn2[:, t, 3, :],
                      V.tensor_scalar(rs_in[:, 0:BT], slot_ap(f"var2_{t}")[:, 0:BT], GN2_EPS, None, ALU.add))
                leave(f"var2_{t}")
                signal(stt(gn2[:, t, 4, :], gn2[:, t, 0, :], -1.0, gn2[:, t, 3, :], ALU.mult, ALU.mult),
                       norm_ready, t + 1)

            def normalise(t):
                wait_job(dve, f"th_{t}_1")
                x1 = coef[:, t, 2, :].rearrange("p (j b h) -> p j b h", b=BT, h=H)
                to = odd_pairs(t).rearrange("p (j b h) -> p j b h", b=BT, h=H)
                for k, b in [(0, b) for b in range(BT)] + [(1, BT - 1)]:
                    p = slice(64 * k, 64 * k + 64)
                    V.tensor_scalar(to[64 * (1 - k):64 * (1 - k) + 64, k:k + PAIRS, b, :], x1[p, :, b, :],
                                    gn2[p, t, 3, b:b + 1], gn2[p, t, 4, b:b + 1], ALU.mult, ALU.add)\
                        .then_inc(xn_too, 1)

            def lower_half(t, h):
                dve.wait_ge(xh_ready, 2 * t + h + 1)
                V.tensor_tensor(by_rows(lo[:, :], t, h)[:, :, 1:1 + H], by_rows(odd_pairs(t), t, h),
                                by_rows(hi[:, :], t, h)[:, :, 1:1 + H].bitcast(f32), ALU.subtract).then_inc(xl_ready, 1)

            def output_sum(t, h):
                wait_reader(dve, f"cf_{t}_{h}")
                V.tensor_tensor(part(coef[:, t, 3, :], t, h), part(coef[:, t, 0, :], t, h),
                                part(coef[:, t, 2, :], t, h), ALU.add).then_inc(sum_ready, 1)

            def step(k, t, before=None, then_do=(), at_total=1, at_rest=-1):
                if k == 0:
                    dve.wait_ge(s_halo, 4 * (t + 1))
                else:
                    dve.wait_ge(halo_ready, 4 * states_through(k - 1, t))
                if at_rest < 0:
                    rest(t, k)
                terms = [(AYM, 0, -1), (AYP, 0, 1), (AXM, -1, 0), (AXP, 1, 0)] + [(AE, 0, 0)] * (products_of(k, t) - 4)
                for i, (a, dw, dc) in enumerate(terms):
                    multiply(t, k, a, dw, dc)
                    if i == at_total and before:
                        total(*before)
                    if i == at_rest:
                        rest(t, k)
                    for at, what in then_do:
                        if at == i:
                            what()
                if direct(k, t):
                    spare = wc(coef[:, 0, 6, :])
                    rest_made[t]()
                    then(V.tensor_tensor(spare, wc(coef[:, t, AE, :]), h_at(t, k), ALU.mult))
                    old = h_at(t, k + 1)
                    rest_made[t] = mark(V.tensor_tensor(old, old, spare, ALU.add))

            def bn_bias(t, conv, h):
                name = f"cv_{t}_{conv}_{h}"
                wait_job(dve, name)
                if t:
                    wait_job(dve, f"bk_0_{conv}_1")
                groups = slice(h * (CG // 2), (h + 1) * (CG // 2))
                frees(V.tensor_tensor(half(gT[conv], h).rearrange("p (g r) -> p g r", g=CG // 2),
                                      slot_ap(name).rearrange("p (g r) -> p g r", g=CG // 2),
                                      bnp[:, 1, conv, groups].unsqueeze(2).broadcast_to([128, CG // 2, BT * H]),
                                      ALU.add), name)

            denominator(0)
            scale_s(1)
            bn_bias(0, 0, 0)
            newton(0)
            split_lo(1)
            diffusivities(0)
            ternary()
            divergence(0)
            wait_job(dve, "alpha")
            then(V.reciprocal(wred[:, 5:6], slot_ap("alpha")[:, 1:2]))
            ins = V.tensor_tensor(wred[:, 7:8], slot_ap("alpha")[:, 0:1], wred[:, 5:6], ALU.mult)
            ins.then_inc(alpha_ready, 1)
            dve.wait_ge(alpha_ready, 1)
            leave("alpha")
            channels_made = over_channels(0)
            g_made = scaled_g(0)
            first_centre(0)
            g_made()
            source(0)

            denominator(1)
            channels_made()
            columns_made = plus_columns(0)
            dve.wait_ge(outp_in, 16 * 10)
            ask_rsqrt(V.tensor_scalar(rs_in[:, 0:1], outp[:, 3:4], BN_EPS, None, ALU.add))
            columns_made()
            columns_made = minus_columns(0)
            bn_bias(1, 1, 1)
            newton(1)

            rsqrt(128, 1, outw[:, 0:1])
            then(V.tensor_tensor(outw[:, 2:3], outw[:, 0:1], outp[:, 0:1], ALU.mult))
            then(V.tensor_tensor(outw[:, 1:2], outw[:, 2:3], outp[:, 2:3], ALU.mult))
            signal(V.tensor_tensor(outw[:, 3:4], outp[:, 1:2], outw[:, 1:2], ALU.subtract), outw_ready, 1)

            diffusivities(1)
            columns_made()

            def meanwhile():
                over_channels(1)()
                divergence_taken(1)

            step(0, 0, then_do=((2, meanwhile),))
            g_made = scaled_g(1)
            first_centre(1)
            g_made()
            source(1)
            columns_made = []
            step(1, 0, then_do=((2, lambda: columns_made.append(plus_columns(1))),
                                (3, lambda: (columns_made[0](), columns_made.append(minus_columns(1))))))
            columns_made[1]()
            step(0, 1, before=(0, 1))
            before = None
            for k, t in ORDER[3:-1]:
                step(k, t, before, at_total=0 if direct(k, t) else 1)
                before = (t, k)
            residual(0, lambda: total(*before))
            step(STEPS - 1, 1, None, ((0, lambda: spread(0)), (2, lambda: second_norm(0)), (3, lambda: normalise(0))),
                 at_rest=2)
            lower_half(0, 0)
            total(1, STEPS - 1)
            lower_half(0, 1)
            residual(1)
            spread(1)
            second_norm(1)
            normalise(1)
            output_sum(0, 0)
            lower_half(1, 0)
            lower_half(1, 1)
            output_sum(0, 1)
            for q in range(4):
                output_sum(1, q)

        @blk.tensor
        def _(pe):
            mm = nc.tensor.matmul

            def take(name):
                if uses_before[name]:
                    pe.wait_ge(slot_free[slot_of[name]], uses_before[name])
                return slot_ap(name)

            def small(name, n, lhsT, rhs):
                mm(take(name)[:, 0:n], lhsT, rhs, start=True, stop=True).then_inc(pe_job, 1)

            def turns(name, blocks):
                dst = take(name)
                for j, src in enumerate(blocks):
                    ins = nc.tensor.transpose(dst[:, j * 128:j * 128 + 128], src, ident[:, :])
                ins.then_inc(pe_job, 1)

            def to_depthwise(t, h):
                pe.wait_ge(s_reordered, t + 1)
                turns(f"t2_{t}_{h}", [half(sT[t], h)[:, j * 128:j * 128 + 128] for j in range(CG // 2)])

            def sobel(t, g, h):
                pe.wait_ge(s_lo, t + 1)
                name = f"{('gy', 'gx')[g]}_{t}_{h}"
                dst = take(name)
                taps_w = ((0, 3), (1, 2), (-1, 2)) if g == 0 else ((1, 0), (-1, 1))
                for bank in range(2):
                    w0 = (2 * h + bank) * (BANK // C)
                    pieces = []
                    for dw, m in taps_w:
                        lo_w, hi_w = w0 + dw, w0 + BANK // C + dw
                        if lo_w < 0:
                            pieces += [(1, 0, 7, m), (0, 1, 1, m)]
                        elif hi_w > W:
                            pieces += [(0, lo_w, 7, m), (7, W - 2, 1, m)]
                        else:
                            pieces.append((0, lo_w, 8, m))
                    if pieces[0][2] < 8:
                        pieces.sort(key=lambda piece: -piece[2])
                    last = len(pieces) - 1
                    for i, (to, frm, count, m) in enumerate(pieces):
                        for part in (hi, lo):
                            ins = mm(dst[:, bank * BANK + to * C:bank * BANK + (to + count) * C],
                                     sobel_m[:, m, :], part[:, frm * C:(frm + count) * C],
                                     start=(i == 0 and part is hi), stop=(i == last and part is lo),
                                     skip_group_check=True)
                ins.then_inc(pe_job, 1)

            def depthwise(t, conv, h):
                name = f"cv_{t}_{conv}_{h}"
                pe.wait_ge(taps_m_ready, 2 * (conv + 1))
                pe.wait_ge(taps_m_too, 2 * (conv + 1))
                wait_reader(pe, f"t2_{t}_0")
                wait_reader(pe, f"t2_{t}_1")
                dst = take(name)
                for j in range(CG // 2):
                    cg = h * (CG // 2) + j
                    src = sT[t][:, cg * 128:cg * 128 + 128].rearrange("p (b h) -> p b h", h=H)
                    to = dst[:, j * 128:j * 128 + 128].rearrange("p (b h) -> p b h", h=H)
                    for dy, o, i in ((1, slice(0, H), slice(0, H)), (0, slice(1, H), slice(0, H - 1)),
                                     (2, slice(0, H - 1), slice(1, H))):
                        ins = mm(to[:, :, o], taps_m[:, 48 * conv + 16 * dy + cg, :], src[:, :, i],
                                 start=(dy == 1), stop=(dy == 2))
                ins.then_inc(pe_job, 1)

            def divergence(t):
                pe.wait_ge(minus_ready, 2)
                for h in range(2):
                    wait_reader(pe, f"bk_{t}_0_{h}")
                    wait_reader(pe, f"bk_{t}_1_{h}")
                g, g1, rows = wc(gN[t]), wc(g1N[t]), BANK // C
                for h in range(2):
                    dst = take(f"dv_{t}_{h}")
                    for bank in range(2):
                        w0 = (2 * h + bank) * rows
                        to = dst[:, bank * BANK:(bank + 1) * BANK].rearrange("p (w c) -> p w c", c=C)
                        pieces = []
                        for dw, m in ((-1, ident[:, :]), (1, minus_ident)):
                            if w0 + dw < 0:
                                pieces += [(to[:, 1:, :], g[:, 0:rows - 1, :], m),
                                           (to[:, 0:1, :], g[:, W - 1:W, :], m)]
                            elif w0 + dw + rows > W:
                                pieces += [(to[:, 0:rows - 1, :], g[:, w0 + 1:W, :], m),
                                           (to[:, rows - 1:, :], g[:, 0:1, :], m)]
                            else:
                                pieces.insert(0, (to, g[:, w0 + dw:w0 + dw + rows, :], m))
                        wide = g1[:, w0:w0 + rows, :]
                        pieces += [(to[:, :, 1:], wide[:, :, 0:C - 1], ident[:, :]),
                                   (to[:, :, 0:1], wide[:, :, C - 1:], ident[:, :]),
                                   (to[:, :, 0:C - 1], wide[:, :, 1:], minus_ident),
                                   (to[:, :, C - 1:], wide[:, :, 0:1], minus_ident)]
                        for i, (out_ap, src, m) in enumerate(pieces):
                            ins = mm(out_ap, m, src, start=(i == 0), stop=(i == len(pieces) - 1),
                                     skip_group_check=True)
                    ins.then_inc(pe_job, 1)

            def back(t, conv, h):
                wait_reader(pe, f"cv_{t}_{conv}_{h}")
                turns(f"bk_{t}_{conv}_{h}",
                      [gT[conv][:, cg * 128:cg * 128 + 128] for cg in range(h * (CG // 2), (h + 1) * (CG // 2))])

            summed = [0]

            def start_sum(t):
                pe.wait_ge(minus_ready, 2)
                dst = [take(f"acc_0_{t}_{h}") for h in range(2)]
                for i, (made, m, src) in enumerate(((centre_ready, ident[:, :], h_at(t, 1)),
                                                    (source_ready, six_ident, wc(coef[:, t, FS, :])))):
                    pe.wait_ge(made, t + 1)
                    for q in range(4):
                        mm(dst[q // 2][:, (q % 2) * BANK:(q % 2 + 1) * BANK], m, src[:, q * 8:q * 8 + 8, :],
                           start=(i == 0), stop=False, skip_group_check=True)

            def sum_products(t, k, between=()):
                dst = [take(f"acc_{k}_{t}_{h}") for h in range(2)]
                count = products_of(k, t)
                for i in range(count):
                    pe.wait_ge(product, summed[0] + 1)
                    src = ring[:, summed[0] % RING, :]
                    summed[0] += 1
                    for q in range(4):
                        ins = mm(dst[q // 2][:, (q % 2) * BANK:(q % 2 + 1) * BANK], ident[:, :],
                                 src[:, q * BANK:(q + 1) * BANK], start=(i == 0 and k > 0),
                                 stop=(i == count - 1), skip_group_check=(k == 0))
                        if i == count - 1 and q == 1:
                            ins.then_inc(pe_job, 1)
                    if i < count - 1:
                        ins.then_inc(ring_free, 1)
                    for at, what in between:
                        if at == i:
                            what()
                ins.then_inc(pe_job, 1)

            def paired(t, name, src, h):
                turns(f"{name}_{t}_{h}", [src[:, 2 * j:2 * j + 2, :] for j in range(h * 8, h * 8 + 8)])

            def h_paired(t):
                for h in range(2):
                    wait_reader(pe, f"acc_{STEPS - 1}_{t}_{h}")
                    paired(t, "th", wc(coef[:, t, 3, :]), h)

            def x_paired(t):
                pe.wait_ge(x_again[t], 16)
                for h in range(2):
                    paired(t, "tx", wc(coef[:, t, 1, :]), h)

            def group_mean2(t):
                pe.wait_ge(mv_ready, t + 1)
                small(f"mean2_{t}", BT, pairavg[:, :, :, :].rearrange("p a b c -> p (a b c)"), mv[:, t, :, 0])

            def group_var2(t):
                pe.wait_ge(q_ready, t + 1)
                small(f"var2_{t}", BT, pairavg[:, :, :, :].rearrange("p a b c -> p (a b c)"), gn2[:, t, 2, :])

            def dense(t, i, first=0, last=None):
                banks = 4 // out_parts[t]
                pe.wait_ge(xl_ready, 2 * t + 1 + (i > 0))
                dst = take(f"cf_{t}_{i}") if first == 0 else slot_ap(f"cf_{t}_{i}")
                for bank in range(banks):
                    j0 = 4 * (banks * i + bank)
                    to = dst[:, bank * BANK:(bank + 1) * BANK].rearrange("p (r h) -> p r h", h=H)
                    steps = [(b, dy, half_of) for b in range(2) for dy in range(3) for half_of in (hi, lo)]
                    for n, (b, dy, half_of) in enumerate(steps):
                        if not first <= bank * len(steps) + n < (last or 1000):
                            continue
                        rows = half_of[:, :].rearrange("p (r h) -> p r h", h=HP)
                        ins = mm(to, dense_m[:, b, dy, :], rows[:, (j0 + b) * BT:(j0 + b + 4) * BT, dy:dy + H],
                                 start=(n == 0), stop=(n == len(steps) - 1))
                if last is None:
                    ins.then_inc(pe_job, 1)

            def out_natural(t, i):
                pe.wait_ge(sum_ready, out_parts[0] * t + i + 1)
                src = part(coef[:, t, 3, :], t, i)
                turns(f"tb_{t}_{i}", [src[:, j * 128:j * 128 + 128] for j in range(16 // out_parts[t])])

            blockm = block[:, :, :].rearrange("p a b -> p (a b)")
            spreadm = spread4[:, :, :].rearrange("p a b -> p (a b)")
            pe.wait_ge(spread_ready, 1)
            pe.wait_ge(taps_in, 32)
            small("wtaps", 2 * 9 * CG, spreadm, taps4[:, :, :, :].rearrange("p a k g -> p (a k g)"))
            pe.wait_ge(near_ready, 1)
            pe.wait_ge(xsum_ready, 2)
            mm(take("mean_0")[:, 0:GROUPS], blockm, gsum[:, 0, 0, :], start=True, stop=False)
            mm(slot_ap("mean_0")[:, 0:GROUPS], blockm, gsum[:, 0, 4, :], start=False, stop=True).then_inc(pe_job, 1)
            pe.wait_ge(bn4_ready, 1)
            small("bnrow", 4 * CG, spreadm, bn4o[:, :, :].rearrange("p a g -> p (a g)"))
            pe.wait_ge(vsum_ready, 1)
            small("var_0", GROUPS, blockm, gsum[:, 0, 2, :])
            pe.wait_ge(xsum_ready, 3)
            small("mean_1", GROUPS, blockm, gsum[:, 1, 0, :])
            pe.wait_ge(ident_ready, 1)
            to_depthwise(0, 0)
            to_depthwise(0, 1)
            pe.wait_ge(sobel_m_ready, 4)
            for g in range(2):
                for h in range(2):
                    sobel(0, g, h)
            depthwise(0, 0, 0)
            pe.wait_ge(vsum_ready, 2)
            small("var_1", GROUPS, blockm, gsum[:, 1, 2, :])
            depthwise(0, 0, 1)
            depthwise(0, 1, 0)
            back(0, 0, 0)
            depthwise(0, 1, 1)
            back(0, 0, 1)
            back(0, 1, 0)
            back(0, 1, 1)
            pe.wait_ge(ones_ready, 1)
            pe.wait_ge(wabs_ready, 1)
            small("wsum", 1, ones[:, :], wred[:, 0:1])
            to_depthwise(1, 0)
            to_depthwise(1, 1)
            depthwise(1, 0, 0)
            depthwise(1, 0, 1)
            pe.wait_ge(kept_ready, 1)
            small("alpha", 2, ones[:, :], wred[:, 3:5])
            for g in range(2):
                for h in range(2):
                    sobel(1, g, h)
            depthwise(1, 1, 0)
            back(1, 0, 0)
            depthwise(1, 1, 1)
            back(1, 0, 1)
            back(1, 1, 0)
            back(1, 1, 1)
            start_sum(0)
            divergence(1)
            for k, t in ORDER:
                if (k, t) == (1, 0):
                    start_sum(1)
                if (k, t) == (STEPS - 2, 1):
                    sum_products(t, k, ((0, lambda: h_paired(0)), (1, lambda: x_paired(0))))
                    pe.wait_ge(pairavg_ready, 2)
                    group_mean2(0)
                elif (k, t) == (STEPS - 1, 1):
                    sum_products(t, k, ((0, lambda: group_var2(0)),))
                else:
                    sum_products(t, k)
            pe.wait_ge(dense_m_ready, 6)
            x_paired(1)
            h_paired(1)
            dense(0, 0)
            group_mean2(1)
            dense(0, 1, 0, 4)
            group_var2(1)
            dense(0, 1, 4)
            out_natural(0, 0)
            dense(1, 0)
            dense(1, 1)
            out_natural(0, 1)
            dense(1, 2)
            out_natural(1, 0)
            dense(1, 3)
            for q in range(1, 4):
                out_natural(1, q)
    return nc


_NAMES = ["x", "L0_conv_wg", "L0_conv_wg1", "L0_conv_g_gamma", "L0_conv_g1_gamma", "L0_conv_g_beta", "L0_conv_g1_beta",
          "L0_conv_g_mean", "L0_conv_g1_mean", "L0_conv_g_var", "L0_conv_g1_var", "L0_conv_out_gamma",
          "L0_conv_out_beta", "L0_conv_out_mean", "L0_conv_out_var", "L1_conv_b", "L1_conv_W"]


def kernel(**inputs):
    import numpy as _np
    import concourse.bacc as _bacc
    from concourse import mybir as _mybir
    from concourse.bass_utils import run_bass_kernel_spmd as _run

    nc = _bacc.Bacc("TRN2", target_bir_lowering=False, num_devices=1)
    arrays, ap = {}, {}
    for name in _NAMES:
        a = _np.ascontiguousarray(inputs[name])
        arrays[f"in_{name}"] = a
        ap[name] = nc.dram_tensor(f"in_{name}", a.shape, _mybir.dt.from_np(a.dtype), kind="ExternalInput").ap()
    out = nc.dram_tensor("out", (B, H, W, C), _mybir.dt.float32, kind="ExternalOutput").ap()
    bn_rows = [ap[n].rearrange("(a g) -> a g", g=CG) for n in _NAMES[3:11]]
    out_cols = [ap[n].rearrange("(c o) -> c o", o=1) for n in _NAMES[11:16]]
    network(nc, ap["x"], ap["L0_conv_wg"], ap["L0_conv_wg1"], bn_rows, out_cols, ap["L1_conv_W"], out)
    r = _run(nc, [arrays], core_ids=[0])
    return r.results[0]["out"]
```
